# Optimizing a Trainium2 kernel written in Bass

```python
import numpy as np
import jax
import jax.numpy as jnp

def _softmax(x, axis=-1):
    return jax.nn.softmax(x, axis=axis)

def _gelu(x):
    return jax.nn.gelu(x, approximate=True)

def _silu(x):
    return jax.nn.silu(x)

def _sigmoid(x):
    return jax.nn.sigmoid(x)

def _layernorm(x, axis=-1, eps=1e-05):
    m = jnp.mean(x, axis=axis, keepdims=True)
    v = jnp.var(x, axis=axis, keepdims=True)
    return (x - m) / jnp.sqrt(v + eps)

def _scatter_add(tgt, idx, src, axis=0):
    return tgt.at[idx].add(src)

def _segment_sum(src, seg, n):
    return jax.ops.segment_sum(src, seg, n)
kernel_name = 'mk_adaln_attn_ffn_d1_seqx_r4_1fa18f'

def setup_inputs(seed: int=0):
    np.random.seed(seed)
    _w = jnp.asarray

    def _rec_inputs():
        import jax
        import jax.numpy as jnp
        _rk = jax.random.key(seed)
        x = -0.000125 + 0.9999 * jax.random.normal(jax.random.fold_in(_rk, 1), (32, 256, 256), jnp.float32)
        _lenS = 256 - jax.random.randint(jax.random.fold_in(_rk, 7), (32,), 0, max(1, 256 // 4) + 1, jnp.int32)
        _lenS2 = 256 - jax.random.randint(jax.random.fold_in(_rk, 8), (32,), 0, max(1, 256 // 4) + 1, jnp.int32)
        cond_1024 = 0.00782532 + 1.00527 * jax.random.normal(jax.random.fold_in(_rk, 11), (32, 256), jnp.float32)
        return (x, cond_1024)
    x, cond_1024 = _rec_inputs()

    def _L0_cond_setup():
        import jax, jax.numpy as jnp
        import numpy as np
        INV_SQRT2 = 0.7071067811865476
        key = jax.random.key(seed)
        k1, k2, k3, k4 = jax.random.split(key, 4)
        B, N, d = (8, 1024, 256)
        scale = 1.0 / np.sqrt(d)
        return {'v': jax.random.normal(k1, (B, N, d), dtype=jnp.float32), 'q_pool': jax.random.normal(k2, (B, d), dtype=jnp.float32), 'W1': jax.random.normal(k3, (d, d), dtype=jnp.float32) * scale, 'b1': jnp.zeros((d,), dtype=jnp.float32), 'W2': jax.random.normal(k4, (d, d), dtype=jnp.float32) * scale, 'b2': jnp.zeros((d,), dtype=jnp.float32)}
    _L0_cond_all = _L0_cond_setup()
    _L0_cond_in = {k: v for k, v in _L0_cond_all.items() if k in ('W1', 'b1', 'W2', 'b2')}
    del _L0_cond_all

    def _L0_attn_setup():
        import jax, jax.numpy as jnp
        import numpy as np
        import math
        DIM = 256
        NUM_HEADS = 16
        HEAD_DIM = DIM // NUM_HEADS

        def build_rope_matrix(dim, seq_len):
            position = jnp.arange(seq_len, dtype=jnp.float32)[:, None]
            dim_pair = jnp.arange(0, dim, 2, dtype=jnp.float32)[None, :]
            theta = 10000.0 ** (-dim_pair / dim)
            freqs = position * theta
            return jnp.concatenate([jnp.cos(freqs), jnp.sin(freqs)], axis=-1)

        def apply_rope(x, rope):
            x1, x2 = (x[..., ::2], x[..., 1::2])
            cos = rope[..., ::2]
            sin = rope[..., 1::2]
            return jnp.concatenate([x1 * cos - x2 * sin, x1 * sin + x2 * cos], axis=-1)
        key = jax.random.key(seed)
        ks = jax.random.split(key, 9)
        B, N = (2, 512)
        x = jax.random.normal(ks[0], (B, N, DIM), dtype=jnp.float32)
        bound = math.sqrt(6.0 / (DIM + DIM))

        def w(k):
            return jax.random.uniform(k, (DIM, DIM), jnp.float32, -bound, bound)

        def b(k):
            return jax.random.uniform(k, (DIM,), jnp.float32, -1.0 / math.sqrt(DIM), 1.0 / math.sqrt(DIM))
        return {'x': x, 'Wq': w(ks[1]), 'bq': b(ks[2]), 'Wk': w(ks[3]), 'bk': b(ks[4]), 'Wv': w(ks[5]), 'bv': b(ks[6]), 'Wo': w(ks[7]), 'bo': b(ks[8])}
    _L0_attn_all = _L0_attn_setup()
    _L0_attn_in = {k: v for k, v in _L0_attn_all.items() if k in ('Wq', 'bq', 'Wk', 'bk', 'Wv', 'bv', 'Wo', 'bo')}
    del _L0_attn_all

    def _L0_cond2_setup():
        import jax, jax.numpy as jnp
        import numpy as np
        EPS = 1e-08
        key = jax.random.key(seed)
        ks = jax.random.split(key, 8)
        B, S, D, H = (8, 512, 256, 256)
        scale = 1.0 / np.sqrt(D)
        return {'input_seq': jax.random.normal(ks[0], (B, S, D), dtype=jnp.float32), 'initial_hidden': jax.random.normal(ks[1], (B, H), dtype=jnp.float32), 'W_f': jax.random.normal(ks[2], (H, D), dtype=jnp.float32) * scale, 'b_f': jnp.zeros((H,), dtype=jnp.float32), 'W_i': jax.random.normal(ks[3], (H, D), dtype=jnp.float32) * scale, 'b_i': jnp.zeros((H,), dtype=jnp.float32), 'W_h': jax.random.normal(ks[4], (H, D), dtype=jnp.float32) * scale, 'b_h': jnp.zeros((H,), dtype=jnp.float32)}
    _L0_cond2_all = _L0_cond2_setup()
    _L0_cond2_in = {k: v for k, v in _L0_cond2_all.items() if k in ('W_f', 'b_f', 'W_i', 'b_i', 'W_h', 'b_h')}
    del _L0_cond2_all

    def _L0_ffn_setup():
        import jax, jax.numpy as jnp
        import numpy as np
        H = 256
        I = 512
        E = 8
        K = 2
        B, S = (4, 1024)
        key = jax.random.key(seed)
        ks = jax.random.split(key, 5)
        scale = 0.02
        return {'hidden_states': jax.random.normal(ks[0], (B, S, H), dtype=jnp.float32), 'gate_w': jax.random.normal(ks[1], (H, E), dtype=jnp.float32) * scale, 'gate_proj_w': jax.random.normal(ks[2], (E, H, I), dtype=jnp.float32) * scale, 'up_proj_w': jax.random.normal(ks[3], (E, H, I), dtype=jnp.float32) * scale, 'down_proj_w': jax.random.normal(ks[4], (E, I, H), dtype=jnp.float32) * scale}
    _L0_ffn_all = _L0_ffn_setup()
    _L0_ffn_in = {k: v for k, v in _L0_ffn_all.items() if k in ('gate_w', 'gate_proj_w', 'up_proj_w', 'down_proj_w')}
    del _L0_ffn_all
    return {'x': x, 'cond_1024': cond_1024, 'L0_cond_W1': _L0_cond_in['W1'], 'L0_cond_b1': _L0_cond_in['b1'], 'L0_cond_W2': _L0_cond_in['W2'], 'L0_cond_b2': _L0_cond_in['b2'], 'L0_attn_Wq': _L0_attn_in['Wq'], 'L0_attn_bq': _L0_attn_in['bq'], 'L0_attn_Wk': _L0_attn_in['Wk'], 'L0_attn_bk': _L0_attn_in['bk'], 'L0_attn_Wv': _L0_attn_in['Wv'], 'L0_attn_bv': _L0_attn_in['bv'], 'L0_attn_Wo': _L0_attn_in['Wo'], 'L0_attn_bo': _L0_attn_in['bo'], 'L0_cond2_W_f': _L0_cond2_in['W_f'], 'L0_cond2_b_f': _L0_cond2_in['b_f'], 'L0_cond2_W_i': _L0_cond2_in['W_i'], 'L0_cond2_b_i': _L0_cond2_in['b_i'], 'L0_cond2_W_h': _L0_cond2_in['W_h'], 'L0_cond2_b_h': _L0_cond2_in['b_h'], 'L0_ffn_gate_w': _L0_ffn_in['gate_w'], 'L0_ffn_gate_proj_w': _L0_ffn_in['gate_proj_w'], 'L0_ffn_up_proj_w': _L0_ffn_in['up_proj_w'], 'L0_ffn_down_proj_w': _L0_ffn_in['down_proj_w']}

def reference(x, cond_1024, L0_cond_W1, L0_cond_b1, L0_cond_W2, L0_cond_b2, L0_attn_Wq, L0_attn_bq, L0_attn_Wk, L0_attn_bk, L0_attn_Wv, L0_attn_bv, L0_attn_Wo, L0_attn_bo, L0_cond2_W_f, L0_cond2_b_f, L0_cond2_W_i, L0_cond2_b_i, L0_cond2_W_h, L0_cond2_b_h, L0_ffn_gate_w, L0_ffn_gate_proj_w, L0_ffn_up_proj_w, L0_ffn_down_proj_w):
    import jax
    import jax.numpy as jnp

    def _L0_cond_ref(v, q_pool, W1, b1, W2, b2):
        import jax, jax.numpy as jnp
        import numpy as np
        INV_SQRT2 = 0.7071067811865476
        B, N, d = v.shape
        h = jax.nn.silu(q_pool @ W1.T + b1)
        gate = jax.nn.sigmoid(h @ W2.T + b2)[:, None, :]
        levels = int(np.log2(N))
        a = v
        details = []
        for _ in range(levels):
            e, o = (a[:, 0::2], a[:, 1::2])
            details.append((e - o) * INV_SQRT2)
            a = (e + o) * INV_SQRT2
        a = a * gate
        for dc in reversed(details):
            dc = dc * gate
            e = (a + dc) * INV_SQRT2
            o = (a - dc) * INV_SQRT2
            n = e.shape[1]
            a = jnp.stack([e, o], axis=2).reshape(B, 2 * n, d)
        return v + a

    def _L0_attn_ref(x, Wq, bq, Wk, bk, Wv, bv, Wo, bo):
        import jax, jax.numpy as jnp
        import numpy as np
        import math
        DIM = 256
        NUM_HEADS = 16
        HEAD_DIM = DIM // NUM_HEADS

        def build_rope_matrix(dim, seq_len):
            position = jnp.arange(seq_len, dtype=jnp.float32)[:, None]
            dim_pair = jnp.arange(0, dim, 2, dtype=jnp.float32)[None, :]
            theta = 10000.0 ** (-dim_pair / dim)
            freqs = position * theta
            return jnp.concatenate([jnp.cos(freqs), jnp.sin(freqs)], axis=-1)

        def apply_rope(x, rope):
            x1, x2 = (x[..., ::2], x[..., 1::2])
            cos = rope[..., ::2]
            sin = rope[..., 1::2]
            return jnp.concatenate([x1 * cos - x2 * sin, x1 * sin + x2 * cos], axis=-1)
        B, N, _ = x.shape
        H, hd = (NUM_HEADS, HEAD_DIM)
        rope = build_rope_matrix(hd, N)

        def proj(W, bias):
            y = x @ W.T + bias
            return y.reshape(B, N, H, hd).transpose(0, 2, 1, 3)
        q = apply_rope(proj(Wq, bq), rope)
        k = apply_rope(proj(Wk, bk), rope)
        v = apply_rope(proj(Wv, bv), rope)
        scores = jnp.einsum('bhqd,bhkd->bhqk', q, k) / math.sqrt(hd)
        probs = jax.nn.softmax(scores, axis=-1)
        out = jnp.einsum('bhqk,bhkd->bhqd', probs, v)
        out = apply_rope(out, -rope)
        out = out.transpose(0, 2, 1, 3).reshape(B, N, DIM)
        return out @ Wo.T + bo

    def _L0_cond2_ref(input_seq, initial_hidden, W_f, b_f, W_i, b_i, W_h, b_h):
        import jax, jax.numpy as jnp
        import numpy as np
        EPS = 1e-08
        forget_gate = jax.nn.sigmoid(jnp.einsum('bsd,hd->bsh', input_seq, W_f) + b_f)
        input_gate = jax.nn.sigmoid(jnp.einsum('bsd,hd->bsh', input_seq, W_i) + b_i)
        gate_sum = forget_gate + input_gate + EPS
        forget_norm = forget_gate / gate_sum
        input_norm = input_gate / gate_sum
        candidate = jnp.einsum('bsd,hd->bsh', input_seq, W_h) + b_h
        new_info = input_norm * candidate
        log_ret = jnp.log(forget_norm + EPS)
        log_cumprod = jnp.cumsum(log_ret, axis=1)
        B, _, H = log_cumprod.shape
        padded = jnp.concatenate([jnp.zeros((B, 1, H), dtype=log_cumprod.dtype), log_cumprod], axis=1)
        scaling = jnp.exp(log_cumprod[:, -1:, :] - padded[:, :-1, :])
        hidden = jnp.cumsum(scaling * new_info, axis=1)
        hidden = hidden + jnp.exp(log_cumprod) * initial_hidden[:, None, :]
        return hidden

    def _L0_ffn_ref(hidden_states, gate_w, gate_proj_w, up_proj_w, down_proj_w):
        import jax, jax.numpy as jnp
        import numpy as np
        H = 256
        I = 512
        E = 8
        K = 2
        B, S = (4, 1024)
        b, s, h = hidden_states.shape
        x = hidden_states.reshape(-1, h)
        T = x.shape[0]
        logits = x @ gate_w
        probs = jax.nn.softmax(logits, axis=-1)
        topk_w, topk_idx = jax.lax.top_k(probs, K)
        topk_w = topk_w / jnp.sum(topk_w, axis=-1, keepdims=True)
        combine = jnp.zeros((T, E), dtype=x.dtype).at[jnp.arange(T)[:, None], topk_idx].add(topk_w)
        out = jnp.zeros_like(x)
        for e in range(E):
            g = jax.nn.silu(x @ gate_proj_w[e])
            u = x @ up_proj_w[e]
            y = g * u @ down_proj_w[e]
            out = out + y * combine[:, e:e + 1]
        return out.reshape(b, s, h)
    x = x + _L0_attn_ref(_L0_cond_ref(x, cond_1024, L0_cond_W1, L0_cond_b1, L0_cond_W2, L0_cond_b2), L0_attn_Wq, L0_attn_bq, L0_attn_Wk, L0_attn_bk, L0_attn_Wv, L0_attn_bv, L0_attn_Wo, L0_attn_bo)
    x = x + _L0_ffn_ref(_L0_cond2_ref(x, cond_1024, L0_cond2_W_f, L0_cond2_b_f, L0_cond2_W_i, L0_cond2_b_i, L0_cond2_W_h, L0_cond2_b_h), L0_ffn_gate_w, L0_ffn_gate_proj_w, L0_ffn_up_proj_w, L0_ffn_down_proj_w)
    return x

_drawn_inputs = setup_inputs


def setup_inputs(seed=0):
    import zlib

    import numpy as np

    out = dict(_drawn_inputs(seed))
    spreads = {'L0_cond_b1': (0.0, 0.564),
     'L0_cond_b2': (0.0, 0.41),
     'L0_cond2_b_f': (0.0, 0.8),
     'L0_cond2_b_i': (0.0, 0.8),
     'L0_cond2_b_h': (0.0, 0.8)}
    factors = {'L0_attn_bq': 2.815,
     'L0_attn_bk': 3.685,
     'L0_cond2_W_f': 8.0,
     'L0_cond2_W_i': 8.0,
     'L0_cond2_W_h': 8.0,
     'L0_ffn_gate_w': 8.0,
     'L0_ffn_gate_proj_w': 8.0,
     'L0_ffn_up_proj_w': 8.0,
     'L0_ffn_down_proj_w': 8.0}
    for name, (base, spread) in spreads.items():
        noise = np.random.default_rng([zlib.crc32(name.encode()), seed]).standard_normal(out[name].shape)
        drawn = base * np.exp(spread * noise) if base else spread * noise
        out[name] = jnp.asarray(drawn.astype(out[name].dtype))
    for name, factor in factors.items():
        out[name] = (out[name] * factor).astype(out[name].dtype)
    return out
```

```python
from contextlib import ExitStack

import numpy as np

import concourse.bass as bass
from concourse import mybir

F32 = mybir.dt.float32
BF16 = mybir.dt.bfloat16
I32 = mybir.dt.int32
U32 = mybir.dt.uint32
ALU = mybir.AluOpType
ACT = mybir.ActivationFunctionType
AX = mybir.AxisListType

P = 128
NB, NT, D = 32, 256, 256
NH, HD = 16, 16
HALF = HD // 2
NE, FF = 8, 512
TOKENS = NB * NT
EPS = 1e-8
SCALE = 1.0 / HD ** 0.5

SPLIT_ROWS = 6 * HD
SCORE_ROWS = SPLIT_ROWS + 2

ROW = 272
ROW_W, ROW_ID = D, D + NE
REGION = TOKENS + P
PAD_ROW = NE * REGION
SORTED = PAD_ROW + P
XBUF = 4
BLOCKS = 2 * TOKENS // P + NE - 1

NBLK = -(-BLOCKS // XBUF) * XBUF

STAGES = {"y": 0, "qk": 1, "max": 2, "att": 3, "out": 4, "rec": 5, "route": 6}
DEPTH = max(STAGES.values())
STEPS = NB + DEPTH
LOOP_FROM, LOOP_TO = DEPTH + 2, NB
UNROLL = 2
N_IN_LOOP = (LOOP_TO - LOOP_FROM) // UNROLL

V_STEPS = 37

JOBS = [("f", "rec"), ("i", "rec"), ("q", "qk"), ("pv3", "out"), ("tr0", "out"), ("tr1", "out"),
        ("k", "qk"), ("pv0", "att"), ("h", "rec"), ("v", "max"), ("pv1", "att"), ("aro", "out"),
        ("rank", "route"), ("wo", "out"), ("x1", "rec"), ("pv2", "att"), ("mt", "max"),
        ("hid", "rec"), ("lg", "rec"), (None, None)]


class Batch:

    def __init__(self, i, offset, count=NB, cycle=UNROLL):
        self.par, self.index, self.turn = offset % cycle, offset, offset // cycle
        if i is not None:
            self.index, self.turn = i * cycle + offset, i + offset // cycle
        self.i, self.offset, self.count, self.cycle = i, offset, count, cycle

    def back(self, n):
        return Batch(self.i, self.offset - n, self.count, self.cycle)

    @property
    def there(self):
        return self.i is not None or 0 <= self.offset < self.count

    def has(self, n):
        return self.i is not None or self.offset >= n


class Step:

    def __init__(self, i, offset):
        self.i, self.offset = i, offset

    def batch(self, stage, before=0):
        return Batch(self.i, self.offset - before - STAGES[stage])


class Event:

    def __init__(self, sem, per=1):
        self.sem, self.per = sem, per

    def of(self, batch, k=None):
        return batch.index * self.per + (self.per if k is None else k)


class Transfer:

    def __init__(self, sems, per=1):
        self.sems, self.per = sems, per

    def of(self, batch):
        return (batch.turn + 1) * (16 * self.per)


class Count:

    def __init__(self):
        self.base, self.n, self.i, self.per = 0, 0, None, 0

    def enter(self, i, per):
        self.base, self.n, self.i, self.per = self.base + self.n, 0, i, per

    def leave(self, times):
        assert self.n == self.per, (self.n, self.per)
        self.base, self.n, self.i = self.base + self.per * times, 0, None

    def up(self, n):
        self.n += n
        value = self.base + self.n
        return value if self.i is None else self.i * self.per + value


def rope_tables():
    position = np.arange(NT, dtype=np.float32)[:, None]
    pair = np.arange(0, HD, 2, dtype=np.float32)[None, :]
    freqs = position * (np.float32(10000.0) ** (-pair / np.float32(HD)))
    rope = np.concatenate([np.cos(freqs), np.sin(freqs)], axis=-1).astype(np.float32)
    return rope[:, ::2], rope[:, 1::2]


def build(nc, xT, condT, w1T, b1, w2T, b2, wqT, bq, wkT, bk, wvT, bv, woT, bo, wfT, bf, wiT, bi, whT, bh,
          gate_w, w_gate, w_up, w_down, rope_qk, rope_v, rope_out, constants, block_numbers, out):
    with ExitStack() as ctx:
        def sb(name, shape, dt=F32):
            return ctx.enter_context(nc.sbuf_tensor(name, shape, dt))

        def sem(name):
            return ctx.enter_context(nc.semaphore(name))

        def event(name, per=1):
            return Event(sem(name), per)

        def transfer(name, per=1, cycle=UNROLL):
            return Transfer([sem(f"{name}{p}") for p in range(cycle)], per)

        q_parts = nc.dram_tensor("q_parts", (6, P, NT), BF16).ap()
        k_parts = nc.dram_tensor("k_parts", (6, P, NT), BF16).ap()
        sorted_rows = nc.dram_tensor("sorted_rows", (SORTED, ROW), F32).ap()

        wo, wf, wi, wh = (sb(f"{n}_sb", [P, 2, D]) for n in ("wo", "wf", "wi", "wh"))
        gw = sb("gw", [P, 2, NE])
        wg_all = sb("wg_all", [P, NE * 2 * FF])
        scores_mem = sb("scores_mem", [P, NE * 4 * D])
        wd_all = scores_mem
        stage_mem = sb("stage_mem", [P, NE * 2 * FF])
        wu_all = stage_mem
        att_mem = sb("att_mem", [P, 18 * 2 * NT])

        def over(mem):
            used = [0]

            def cut(shape, dt=F32):
                n = int(np.prod(shape))
                words = n if dt != BF16 else n // 2
                view = mem[:, used[0]:used[0] + words]
                used[0] += words
                assert used[0] <= mem.shape[1], (used[0], mem.shape)
                view = view if dt == F32 else view.bitcast(dt)
                names = "abcd"[:len(shape)]
                return view.rearrange(f"p ({' '.join(names)}) -> p {' '.join(names)}", **dict(zip(names, shape)))
            return cut

        bias = sb("bias", [P, 7, 2])
        bias12 = sb("bias12", [P, 2, 2])
        bv_sb = sb("bv_sb", [P, D])
        rv = sb("rv", [P, 2, 2 * D])
        ro = sb("ro", [P, 2, 2 * D])
        cst = sb("cst", [P, 3 * P + 64])
        ident, upper, ones = cst[:, 0:P], cst[:, P:2 * P], cst[:, 2 * P:3 * P]
        iota_e = cst[:, 3 * P:3 * P + NE]
        region_e = cst[:, 3 * P + NE:3 * P + 2 * NE]
        token_p = cst[:, 3 * P + 2 * NE:3 * P + 2 * NE + 2]
        ident_b = sb("ident_b", [P, P], BF16)
        cond_sb = sb("cond_sb", [P, 2, NB])
        g1 = sb("g1", [P, 2, NB])
        gh = sb("gh", [P, 2, NB])
        gs = sb("gs", [P, 2, NB])
        ones_row = sb("ones_row", [P, NT])
        eps_sb = sb("eps_sb", [P, 1])

        early = over(stage_mem)
        wq, wk, wv = early([2, D]), early([2, D]), early([2, D])
        rqk = early([2, 2 * NT])
        x_in = early([2, NT])
        x_res = sb("x_res", [P, 2, NT])
        y = early([2, 2, NT])
        q_lin, k_lin = early([2 * NT]), early([2 * NT])
        t1, t2 = sb("t1", [P, 2 * NT]), sb("t2", [P, 2 * NT])
        q_rope, k_rope = early([2 * NT]), early([2 * NT])
        q_split, k_split = early([3, 2 * NT], BF16), early([3, 2 * NT], BF16)
        rest = early([2 * NT])
        operands = over(scores_mem)
        q_rows, k_rows = operands([2, NH, NT], BF16), operands([2, NH, NT], BF16)
        attention = over(att_mem)
        probs = attention([8, 2, NT])
        v_aug = attention([2, 2 * NH, 2 * HD])
        v_lin = attention([2 * D])
        mx = sb("mx", [P, 2, NH])
        mx_split = sb("mx_split", [P, 2, 2, NH], BF16)
        mx_rows = sb("mx_rows", [2 * NH, NT], BF16)
        o_raw = attention([4, NT])
        o_den = sb("o_den", [P, 2, NH])
        o_norm, o_rope, o_T = attention([2, D]), attention([2, D]), attention([2, NT])
        x1 = sb("x1", [P, 2, 2, NT])
        x1_row = sb("x1_row", [P, 2, D])
        fg, ig = sb("fg", [P, 2, NT]), sb("ig", [P, 2, NT])
        rc = sb("rc", [P, 2, NT])
        lr = sb("lr", [P, 2, NT])
        lc = sb("lc", [P, 2, NT + 1])
        scaling = sb("scaling", [P, 2, NT])
        decay = sb("decay", [P, 2, NT])
        info = sb("info", [P, 2, NT])
        hid = sb("hid", [P, 2, NT])
        hrow = sb("hrow", [P, 2, 2, ROW])
        lg = sb("lg", [P, 2, NE])
        r_a, r_b, r_c, oh1, oh2, comb = (sb(n, [P, 2, NE]) for n in ("r_a", "r_b", "r_c", "oh1", "oh2", "comb"))
        m1, m2, mv, ex, w1c, w2c = (sb(n, [P, 2]) for n in ("m1", "m2", "mv", "ex", "w1c", "w2c"))
        sl = sb("sl", [P, 2, 2])
        oh_b = sb("oh_b", [P, 2, NE])
        slots = sb("slots", [P, 2, 2], U32)
        tid = sb("tid", [P, 2])
        at_e = sb("at_e", [P, NE])

        ps_st = [ctx.enter_context(nc.psum_tensor(f"ps_st{i}", [P, 2, 2, NT], F32)) for i in range(2)]
        ps_sm = [ctx.enter_context(nc.psum_tensor(f"ps_sm{i}", [P, 2, NT], F32)) for i in range(2)]
        ps_job = [ctx.enter_context(nc.psum_tensor(f"ps_job{i}", [P, 512], F32)) for i in range(2)]
        bank = {name: ps_job[n % 2] for n, (name, _) in enumerate(JOBS)}

        consts_in = sem("consts_in")
        setup_done = sem("setup_done")
        experts_in = sem("experts_in")
        gate_pe, gate_act, gate_v = sem("gate_pe"), sem("gate_act"), sem("gate_v")
        x_loaded, res_loaded = transfer("x_loaded"), transfer("res_loaded")
        q_stored, k_stored = transfer("q_stored"), transfer("k_stored")
        rows_loaded = transfer("rows_loaded", 9)
        max_loaded = transfer("max_loaded", 2)
        x1_stored = transfer("x1_stored")
        scattered = transfer("scattered", 4)
        pe = {name: event(f"pe_{name}") for name in
              ("f", "i", "h", "q", "k", "v", "aro", "wo", "x1", "mt", "hid", "lg", "rank")}
        pe_pv, pe_tr, pe_st, pe_sm = event("pe_pv", 4), event("pe_tr", 2), event("pe_st", 8), event("pe_sm", NH)
        a_f, a_i, a_q, a_k, a_ln, a_dec, a_at, a_x1, a_hid, a_re = (
            event(f"a_{n}") for n in ("f", "i", "q", "k", "ln", "dec", "at", "x1", "hid", "re"))
        a_exp, a_ov = event("a_exp", 8), event("a_ov", 4)
        v_y, v_rc, v_cum, v_new, v_v, v_q, v_k, v_mx, v_mt, v_x1, v_hid, v_lg, v_dm, v_oh, v_slot = (
            event(f"v_{n}") for n in
            ("y", "rc", "cum", "new", "v", "q", "k", "mx", "mt", "x1", "hid", "lg", "dm", "oh", "slot"))
        v_max, v_tr = event("v_max", NH), event("v_tr", 2)
        g_q, g_k, g_v, g_o, g_gate = (event(f"g_{n}") for n in ("q", "k", "v", "o", "gate"))
        v_rank = event("v_rank")
        v_steps, g_steps = sem("v_steps"), sem("g_steps")

        evacuated = {"f": (a_f, 1), "i": (a_i, 1), "q": (a_q, 1), "k": (a_k, 1), "h": (v_new, 1), "v": (v_v, 1),
                     "aro": (a_at, 1), "wo": (v_x1, 1), "x1": (a_x1, 1), "mt": (v_mt, 1), "hid": (a_hid, 1),
                     "lg": (v_lg, 1), "rank": (v_rank, 1)}
        for n in range(4):
            evacuated[f"pv{n}"] = (a_ov, n + 1)
        for n in range(2):
            evacuated[f"tr{n}"] = (v_tr, n + 1)

        def bank_free(step, job):
            at = [name for name, _ in JOBS].index(job)
            for n in range(at - 2, at - 2 * len(JOBS), -2):
                name, stage = JOBS[n % len(JOBS)]
                if name is None:
                    continue
                batch = step.batch(stage, before=1 if n < 0 else 0)
                if batch.there:
                    got = evacuated[name]
                    return [(got[0].sem, got[0].of(batch, got[1]))]
            return []

        def all_steps(eng, body, counts=()):
            for t in range(LOOP_FROM):
                body(Step(None, t))
            with eng.Fori(0, N_IN_LOOP) as i:
                for count, per in counts:
                    count.enter(i, per)
                for t in range(UNROLL):
                    body(Step(i, LOOP_FROM + t))
            for count, _ in counts:
                count.leave(N_IN_LOOP)
            for t in range(LOOP_TO, STEPS):
                body(Step(None, t))

        late = over(att_mem)
        xb = late([XBUF, ROW])
        xb_T = late([2, 2, P])
        silu = late([2, FF])
        gu = late([2, FF])
        gu_T = late([4, P])
        ysb = late([2, D])
        wsel, wrow = sb("wsel", [P, NE]), sb("wrow", [P, 2])
        pad_rows = sb("pad_rows", [P, ROW])
        cnt, nblk, endb = sb("cnt", [P, NE]), sb("nblk", [P, NE]), sb("endb", [P, NE])
        cnt_i = sb("cnt_i", [P, NE], I32)
        at_i = sb("at_i", [P, NE], I32)
        blk = sb("blk", [P, NBLK])
        blk_ge, blk_oh = late([NBLK, NE]), late([NBLK, NE])
        blk_e, blk_s = sb("blk_e", [P, NBLK]), sb("blk_s", [P, NBLK])
        row_tab, exp_tab = sb("row_tab", [P, NBLK], I32), sb("exp_tab", [P, NBLK], I32)
        ps_g = [t[:, 0].rearrange("p a t -> p (a t)") for t in ps_st]
        ps_u = [t[:, 1].rearrange("p a t -> p (a t)") for t in ps_st]
        ps_tx = ps_sm[0][:].rearrange("p a t -> p (a t)")
        ps_tg = ps_sm[1][:].rearrange("p a t -> p (a t)")
        ps_y = ps_job
        tables_ready, pads_in, tail_zeroed = sem("tables_ready"), sem("pads_in"), sem("tail_zeroed")
        f_w = sem("f_w")
        pads_made = sem("pads_made")
        xb_in, added = transfer("xb_in", 1, XBUF), transfer("added", 1, XBUF)
        f_tx, f_g, f_u, f_tg, f_y = (event(f"f_{n}") for n in ("tx", "g", "u", "tg", "y"))
        f_xT, f_silu, f_gu, f_guT, f_out = (event(f"f_{n}") for n in ("xT", "silu", "gu", "guT", "out"))

        SETUP_LOADS = [
            (wq[:], wqT), (wk[:], wkT), (wv[:], wvT), (wo[:], woT), (wf[:], wfT), (wi[:], wiT), (wh[:], whT),
            (gw[:], gate_w), (cond_sb[:], condT), (cst[:], constants), (bv_sb[:], bv), (blk[:], block_numbers),
            (rqk[:].rearrange("p a t -> p (a t)"), rope_qk), (rv[:].rearrange("p a t -> p (a t)"), rope_v),
            (ro[:].rearrange("p a t -> p (a t)"), rope_out),
            (bias[:, 0], bq), (bias[:, 1], bk), (bias[:, 2], bo), (bias[:, 3], bf), (bias[:, 4], bi),
            (bias[:, 5], bh), (bias12[:, 0], b1), (bias12[:, 1], b2),
            (probs[:, 0, :, :], w1T), (probs[:, 1, :, :], w2T),
        ]
        CONSTS = 16 * len(SETUP_LOADS)
        w1_sb, w2_sb = probs[:, 0, :, :], probs[:, 1, :, :]
        SETUP_DONE = 7

        def ffn_steps(eng, body, *stages):
            def turn(i, base):
                for k in range(XBUF):
                    body(*(Batch(i, base + k - s, NBLK, XBUF) for s in stages))
            turn(None, 0)
            with eng.Fori(0, NBLK // XBUF - 1) as i:
                turn(i, XBUF)
            if max(stages):
                turn(None, NBLK)

        sp_waits_passed, pool_waits_passed = sem("sp_waits_passed"), sem("pool_waits_passed")

        block = ctx.enter_context(nc.Block())

        @block.sync
        def _(sp):
            for dst, src in SETUP_LOADS:
                sp.dma_start(dst, src).then_inc(consts_in, 16)
            sp.dma_start(wg_all[:], w_gate).then_inc(experts_in, 16)
            sp.wait_ge(pads_made, 1)
            sp.dma_start(sorted_rows[PAD_ROW:PAD_ROW + P, :], pad_rows[:]).then_inc(tail_zeroed, 16)
            sp.dma_start(out[TOKENS:TOKENS + P, :], pad_rows[:, 0:D]).then_inc(tail_zeroed, 16)

            def step(s):
                a, b, m, c, d = (s.batch(n) for n in ("y", "qk", "max", "out", "rec"))
                if a.there:
                    if a.has(1):
                        sp.wait_ge(v_y.sem, v_y.of(a.back(1)))
                    sp.sem_inc(sp_waits_passed, 1)
                    sp.dma_start(
                        x_in[:], xT[:, bass.ds(a.index, 1), :].rearrange("(c p) o t -> p (o c) t", p=P)).then_inc(x_loaded.sems[a.par], 16)
                if c.there:
                    if c.has(1):
                        sp.wait_ge(v_x1.sem, v_x1.of(c.back(1)))
                    sp.sem_inc(sp_waits_passed, 1)
                    sp.dma_start(
                        x_res[:], xT[:, bass.ds(c.index, 1), :].rearrange("(c p) o t -> p (o c) t", p=P)).then_inc(res_loaded.sems[c.par], 16)
                if b.there:
                    if b.has(1):
                        sp.wait_ge(rows_loaded.sems[b.back(1).par], rows_loaded.of(b.back(1)))
                    sp.wait_ge(v_q.sem, v_q.of(b))
                    sp.dma_start(q_parts.rearrange("x p t -> p x t"),
                                                 q_split[:].rearrange("p c (a t) -> p (c a) t", a=2)).then_inc(q_stored.sems[b.par], 16)
                    sp.wait_ge(v_k.sem, v_k.of(b))
                    sp.dma_start(k_parts.rearrange("x p t -> p x t"),
                                                 k_split[:].rearrange("p c (a t) -> p (c a) t", a=2)).then_inc(k_stored.sems[b.par], 16)
                if b.there:
                    if b.has(2):
                        sp.wait_ge(pe_st.sem, pe_st.of(b.back(2)))
                    sp.sem_inc(sp_waits_passed, 1)
                    sp.wait_ge(q_stored.sems[b.par], q_stored.of(b))
                    sp.wait_ge(k_stored.sems[b.par], k_stored.of(b))
                    qv = q_parts.rearrange("x (i h) t -> (x i) (h t)", h=NH)
                    kv = k_parts.rearrange("x (i h) t -> (x i) (h t)", h=NH)
                    row = 0
                    for parts in (3, 2, 1):
                        n = parts * HD
                        sp.dma_start(
                            q_rows[row:row + n, b.par].rearrange("p h t -> p (h t)"), qv[0:n, :]).then_inc(rows_loaded.sems[b.par], 16)
                        row += n
                    for n, part in enumerate((0, 0, 0, 1, 1, 2)):
                        sp.dma_start(
                            k_rows[n * HD:n * HD + HD, b.par].rearrange("p h t -> p (h t)"),
                            kv[part * HD:part * HD + HD, :]).then_inc(rows_loaded.sems[b.par], 16)
                if m.there:
                    if m.has(2):
                        sp.wait_ge(pe_st.sem, pe_st.of(m.back(2)))
                    sp.sem_inc(sp_waits_passed, 1)
                    sp.wait_ge(v_mt.sem, v_mt.of(m))
                    for part in range(2):
                        sp.dma_start(
                            q_rows[SPLIT_ROWS + part:SPLIT_ROWS + part + 1, m.par, :, :],
                            mx_rows[NH * part:NH * part + NH, :]).then_inc(max_loaded.sems[m.par], 16)
                if d.there:
                    sp.wait_ge(a_x1.sem, a_x1.of(d))
                    sp.sem_inc(sp_waits_passed, 1)
                    sp.dma_start(
                        out[bass.ds(d.index * NT, NT), :].rearrange("(c p) f -> p c f", p=P), x1_row[:]).then_inc(x1_stored.sems[d.par], 16)

            all_steps(sp, step)

            sp.wait_ge(pe_st.sem, pe_st.of(Batch(None, NB - 1)))
            sp.wait_ge(pe["v"].sem, pe["v"].of(Batch(None, NB - 1)))
            sp.dma_start(wd_all[:], w_down).then_inc(experts_in, 16)
            sp.dma_start(wu_all[:], w_up).then_inc(experts_in, 16)
            sp.wait_ge(tables_ready, 1)
            for e in range(NE):
                row = sp.value_load(at_i[0:1, e:e + 1], min_val=0, max_val=SORTED - P)
                sp.dma_start(sorted_rows[bass.ds(row, P), :], pad_rows[:]).then_inc(pads_in, 16)
            sp.wait_ge(pads_in, 16 * NE)
            sp.wait_ge(tail_zeroed, 32)
            for n in range(2):
                sp.wait_ge(scattered.sems[Batch(None, NB - 1 - n).par], scattered.of(Batch(None, NB - 1 - n)))
                sp.wait_ge(x1_stored.sems[Batch(None, NB - 1 - n).par], x1_stored.of(Batch(None, NB - 1 - n)))

            def load_block(n):
                if n.has(XBUF):
                    sp.wait_ge(added.sems[n.back(XBUF).par], added.of(n.back(XBUF)))
                sp.sem_inc(sp_waits_passed, 1)
                row = sp.value_load(row_tab[0:1, bass.ds(n.index, 1)], min_val=0, max_val=PAD_ROW)
                sp.dma_start(xb[:, n.par], sorted_rows[bass.ds(row, P), :]).then_inc(xb_in.sems[n.par], 16)

            for k in range(XBUF):
                load_block(Batch(None, k, NBLK, XBUF))
            with sp.Fori(0, NBLK // XBUF - 1) as i:
                for k in range(XBUF):
                    load_block(Batch(i, XBUF + k, NBLK, XBUF))
            for k in range(XBUF):
                sp.wait_ge(added.sems[k], 16 * NBLK // XBUF)

        @block.gpsimd
        def _(pool):
            steps = Count()

            def products(x, tables):
                pool.tensor_tensor(t1[:], x, tables[:, 0], ALU.mult).then_inc(g_steps, 1)
                pool.tensor_tensor(t2[:], x, tables[:, 1], ALU.mult).then_inc(g_steps, 1)
                pool.wait_ge(g_steps, steps.up(2))

            def rope_by_feature(x, to, event, batch):
                products(x, rqk)
                pool.tensor_tensor(to[:, 0:NT], t1[:, 0:NT], t1[:, NT:], ALU.subtract).then_inc(g_steps, 1)
                pool.tensor_tensor(to[:, NT:], t2[:, 0:NT], t2[:, NT:], ALU.add).then_inc(event.sem, 1)
                pool.wait_ge(g_steps, steps.up(1))
                pool.wait_ge(event.sem, event.of(batch))

            def step(s):
                b, m, c, d, e = (s.batch(n) for n in ("qk", "max", "out", "rec", "route"))
                if b.there:
                    pool.wait_ge(a_q.sem, a_q.of(b))
                    if b.has(1):
                        pool.wait_ge(v_q.sem, v_q.of(b.back(1)))
                    rope_by_feature(q_lin[:], q_rope, g_q, b)
                if d.there:
                    pool.wait_ge(v_rc.sem, v_rc.of(d))
                    pool.tensor_tensor(fg[:], fg[:], rc[:], ALU.mult)
                    pool.tensor_tensor(ig[:], ig[:], rc[:], ALU.mult).then_inc(g_gate.sem, 1)
                if c.there:
                    pool.wait_ge(v_tr.sem, v_tr.of(c))
                    products(o_norm[:].rearrange("p c f -> p (c f)"), ro)
                    if c.has(1):
                        pool.wait_ge(pe["aro"].sem, pe["aro"].of(c.back(1)))
                    to = o_rope[:].rearrange("p c (h a i) -> p (c h) a i", h=NH, a=2)
                    t1v, t2v = (t[:].rearrange("p (g i a) -> p g i a", i=HALF, a=2) for t in (t1, t2))
                    pool.tensor_tensor(to[:, :, 0], t1v[:, :, :, 0], t1v[:, :, :, 1], ALU.add).then_inc(g_steps, 1)
                    pool.tensor_tensor(to[:, :, 1], t2v[:, :, :, 0], t2v[:, :, :, 1], ALU.add).then_inc(g_o.sem, 1)
                    pool.wait_ge(g_steps, steps.up(1))
                    pool.wait_ge(g_o.sem, g_o.of(c))
                if b.there:
                    pool.wait_ge(a_k.sem, a_k.of(b))
                    if b.has(1):
                        pool.wait_ge(v_k.sem, v_k.of(b.back(1)))
                    rope_by_feature(k_lin[:], k_rope, g_k, b)
                if m.there:
                    pool.wait_ge(v_v.sem, v_v.of(m))
                    products(v_lin[:], rv)
                    if m.has(2):
                        pool.wait_ge(pe_pv.sem, pe_pv.of(m.back(2)))
                    va = v_aug[:, m.par].rearrange("p (c h) k -> p c h k", c=2)
                    t1v, t2v = (t[:].rearrange("p (c a h i) -> p c a h i", c=2, a=2, i=HALF) for t in (t1, t2))
                    pool.tensor_tensor(va[:, :, :, 0:HALF], t1v[:, :, 0], t1v[:, :, 1],
                                                    ALU.subtract).then_inc(g_steps, 1)
                    pool.tensor_tensor(va[:, :, :, HALF:HD], t2v[:, :, 0], t2v[:, :, 1],
                                                  ALU.add).then_inc(g_v.sem, 1)
                    pool.wait_ge(g_steps, steps.up(1))
                    pool.wait_ge(g_v.sem, g_v.of(m))
                if e.there:
                    pool.wait_ge(v_slot.sem, v_slot.of(e))
                    pool.wait_ge(a_hid.sem, a_hid.of(e))
                    pool.sem_inc(pool_waits_passed, 1)
                    for choice in range(2):
                        for tc in range(2):
                            pool.indirect_dma_start(
                                out=sorted_rows, out_offset=bass.IndirectOffsetOnAxis(
                                    ap=slots[:, choice, tc:tc + 1], axis=0),
                                in_=hrow[:, e.par, tc], in_offset=None).then_inc(scattered.sems[e.par], 16)

            pool.wait_ge(consts_in, CONSTS)
            pool.wait_ge(setup_done, SETUP_DONE)
            all_steps(pool, step, [(steps, 4 * UNROLL * 3)])

            pool.wait_ge(tail_zeroed, 32)
            for n in range(2):
                pool.wait_ge(x1_stored.sems[Batch(None, NB - 1 - n).par], x1_stored.of(Batch(None, NB - 1 - n)))

            def add_block(n):
                pool.wait_ge(f_out.sem, f_out.of(n))
                if n.has(1):
                    pool.wait_ge(added.sems[n.back(1).par], added.of(n.back(1)))
                pool.sem_inc(pool_waits_passed, 1)
                pool.indirect_dma_start(
                    out=out, out_offset=bass.IndirectOffsetOnAxis(
                        ap=xb[:, n.par, ROW_ID:ROW_ID + 1].bitcast(U32), axis=0),
                    in_=ysb[:, n.par % 2], in_offset=None, compute_op=ALU.add).then_inc(added.sems[n.par], 16)

            for k in range(XBUF):
                add_block(Batch(None, k, NBLK, XBUF))
            with pool.Fori(0, NBLK // XBUF - 1) as i:
                for k in range(XBUF):
                    add_block(Batch(i, XBUF + k, NBLK, XBUF))

        @block.scalar
        def _(act):
            act.wait_ge(consts_in, CONSTS)
            act.wait_ge(gate_pe, 1)
            for c in range(2):
                act.activation(gh[:, c], ps_job[0][:, c * NB:c * NB + NB], ACT.Identity, bias=bias12[:, 0, c:c + 1])
            for c in range(2):
                act.activation(gs[:, c], ps_job[0][:, c * NB:c * NB + NB], ACT.Sigmoid,
                               bias=bias12[:, 0, c:c + 1]).then_inc(gate_act, 1)
            act.wait_ge(gate_pe, 2)
            for c in range(2):
                act.activation(g1[:, c], ps_job[1][:, c * NB:c * NB + NB], ACT.Sigmoid,
                               bias=bias12[:, 1, c:c + 1]).then_inc(gate_act, 1)

            def by_feature(to, frm, func, b):
                for c in range(2):
                    last = act.activation(to[:, c * NT:c * NT + NT], frm[:, c * NT:c * NT + NT], func, bias=bias[:, b, c:c + 1])
                return last

            def exp(s, u):
                if s.there:
                    act.wait_ge(pe_st.sem, pe_st.of(s, u + 1))
                    if u >= 4:
                        act.wait_ge(pe_pv.sem, pe_pv.of(s, (u - 4) // 2 + 1))
                    else:
                        if s.has(1):
                            act.wait_ge(pe_pv.sem, pe_pv.of(s.back(1), 3 + u // 2))
                    at = 2 * u % 8
                    act.activation(probs[:, at:at + 2], ps_st[u % 2][:], ACT.Exp, scale=SCALE).then_inc(a_exp.sem, 1)

            def outputs(b, g):
                if b.there:
                    act.wait_ge(pe_pv.sem, pe_pv.of(b, g + 1))
                    if b.has(1):
                        act.wait_ge(pe_tr.sem, pe_tr.of(b.back(1)))
                    act.copy(o_raw[:, g], bank[f"pv{g}"][:, 0:NT]).then_inc(a_ov.sem, 1)

            def step(s):
                b, a, c, d, e = (s.batch(n) for n in ("qk", "att", "out", "rec", "route"))
                if d.there:
                    act.wait_ge(pe["f"].sem, pe["f"].of(d))
                    if d.has(1):
                        act.wait_ge(a_ln.sem, a_ln.of(d.back(1)))
                    by_feature(fg[:].rearrange("p c t -> p (c t)"), bank["f"], ACT.Sigmoid, 3).then_inc(a_f.sem, 1)
                    act.wait_ge(pe["i"].sem, pe["i"].of(d))
                    if d.has(1):
                        act.wait_ge(v_new.sem, v_new.of(d.back(1)))
                    by_feature(ig[:].rearrange("p c t -> p (c t)"), bank["i"], ACT.Sigmoid, 4).then_inc(a_i.sem, 1)
                if b.there:
                    act.wait_ge(pe["q"].sem, pe["q"].of(b))
                    if b.has(1):
                        act.wait_ge(g_q.sem, g_q.of(b.back(1)))
                    by_feature(q_lin, bank["q"], ACT.Identity, 0).then_inc(a_q.sem, 1)
                outputs(c, 3)
                exp(a, 0)
                exp(a, 1)
                if b.there:
                    act.wait_ge(pe["k"].sem, pe["k"].of(b))
                    if b.has(1):
                        act.wait_ge(g_k.sem, g_k.of(b.back(1)))
                    by_feature(k_lin, bank["k"], ACT.Identity, 1).then_inc(a_k.sem, 1)
                exp(a, 2)
                outputs(a, 0)
                if d.there:
                    act.wait_ge(g_gate.sem, g_gate.of(d))
                    if d.has(1):
                        act.wait_ge(v_cum.sem, v_cum.of(d.back(1)))
                    act.activation(lr[:], fg[:], ACT.Ln, bias=eps_sb[:, 0:1]).then_inc(a_ln.sem, 1)
                exp(a, 3)
                if d.there:
                    act.wait_ge(v_cum.sem, v_cum.of(d))
                    if d.has(1):
                        act.wait_ge(v_hid.sem, v_hid.of(d.back(1)))
                    for k in range(2):
                        act.activation(scaling[:, k], lc[:, k, 0:NT], ACT.Exp, scale=-1.0, bias=lc[:, k, NT:NT + 1])
                    act.activation(decay[:], lc[:, :, 1:NT + 1], ACT.Exp).then_inc(a_dec.sem, 1)
                exp(a, 4)
                outputs(a, 1)
                if c.there:
                    act.wait_ge(pe["aro"].sem, pe["aro"].of(c))
                    if c.has(1):
                        act.wait_ge(pe["wo"].sem, pe["wo"].of(c.back(1)))
                    act.copy(o_T[:].rearrange("p c t -> p (c t)"), bank["aro"][:, 0:2 * NT]).then_inc(a_at.sem, 1)
                exp(a, 5)
                if e.there:
                    act.wait_ge(v_dm.sem, v_dm.of(e))
                    act.activation(ex[:], ex[:], ACT.Exp).then_inc(a_re.sem, 1)
                exp(a, 6)
                if d.there:
                    act.wait_ge(pe["x1"].sem, pe["x1"].of(d))
                    if d.has(1):
                        act.wait_ge(x1_stored.sems[d.back(1).par], x1_stored.of(d.back(1)))
                    act.copy(x1_row[:].rearrange("p c t -> p (c t)"), bank["x1"][:, 0:2 * NT]).then_inc(a_x1.sem, 1)
                outputs(a, 2)
                exp(a, 7)
                if d.there:
                    act.wait_ge(pe["hid"].sem, pe["hid"].of(d))
                    if d.has(2):
                        act.wait_ge(scattered.sems[d.back(2).par], scattered.of(d.back(2)))
                    act.copy(hrow[:, d.par, :, 0:D], bank["hid"][:, 0:2 * NT].rearrange("p (c f) -> p c f", c=2)).then_inc(a_hid.sem, 1)

            act.wait_ge(setup_done, SETUP_DONE)
            all_steps(act, step)

            def ffn(n_g, n_t):
                if n_t.there:
                    act.wait_ge(f_tg.sem, f_tg.of(n_t))
                    if n_t.has(1):
                        act.wait_ge(f_y.sem, f_y.of(n_t.back(1)))
                    act.copy(gu_T[:].rearrange("p a t -> p (a t)"), ps_tg).then_inc(f_guT.sem, 1)
                if n_g.there:
                    act.wait_ge(f_g.sem, f_g.of(n_g))
                    if n_g.has(2):
                        act.wait_ge(f_gu.sem, f_gu.of(n_g.back(2)))
                    act.activation(silu[:, n_g.par % 2], ps_g[n_g.par % 2], ACT.Silu).then_inc(f_silu.sem, 1)

            ffn_steps(act, ffn, 0, 1)

        @block.vector
        def _(v):
            steps = Count()

            def tt(o, a, b, op):
                return v.tensor_tensor(o, a, b, op)

            v.memset(ones_row[:], 1.0).then_inc(setup_done, 1)
            v.memset(eps_sb[:], EPS).then_inc(setup_done, 1)
            v.memset(v_aug.rearrange("p a g k -> p (a g) k")[:, :, HD:], 1.0).then_inc(setup_done, 1)
            v.memset(k_rows[SPLIT_ROWS:SCORE_ROWS], -1.0).then_inc(setup_done, 1)
            v.memset(lc[:, :, 0:1], 0.0).then_inc(setup_done, 1)
            v.memset(hrow[:], 0.0).then_inc(setup_done, 1)
            v.memset(pad_rows[:], 0.0).then_inc(gate_v, 1)
            v.wait_ge(consts_in, CONSTS)
            v.tensor_copy(ident_b[:], ident).then_inc(gate_v, 1)
            v.tensor_copy(tid[:], token_p).then_inc(gate_v, 1)
            v.tensor_copy(at_e[:], region_e).then_inc(gate_v, 1)
            v.wait_ge(gate_v, 4)
            v.tensor_scalar(pad_rows[:, ROW_ID:ROW_ID + 1].bitcast(U32), tid[:, 0:1], float(TOKENS), None,
                            ALU.add).then_inc(pads_made, 1)
            v.wait_ge(gate_act, 2)
            tt(gh[:], gh[:], gs[:], ALU.mult).then_inc(gate_v, 1)
            v.wait_ge(gate_act, 4)
            v.tensor_scalar(g1[:], g1[:], 1.0, None, ALU.add).then_inc(setup_done, 1)
            v.wait_ge(setup_done, SETUP_DONE)
            v.wait_ge(pads_made, 1)

            def row_max(m, h):
                if m.there:
                    if h == 0 and m.has(1):
                        v.wait_ge(v_mx.sem, v_mx.of(m.back(1)))
                    v.wait_ge(pe_sm.sem, pe_sm.of(m, h + 1))
                    v.tensor_reduce(mx[:, :, h], ps_sm[h % 2][:], AX.X, ALU.max).then_inc(v_max.sem, 1)

            def split(b, x, to, ready, stored, done):
                v.wait_ge(ready.sem, ready.of(b))
                if b.has(1):
                    v.wait_ge(stored.sems[b.back(1).par], stored.of(b.back(1)))
                v.tensor_copy(to[:, 0], x[:]).then_inc(v_steps, 1)
                v.wait_ge(v_steps, steps.up(1))
                tt(rest[:], x[:], to[:, 0], ALU.subtract).then_inc(v_steps, 1)
                v.wait_ge(v_steps, steps.up(1))
                v.tensor_copy(to[:, 1], rest[:]).then_inc(v_steps, 1)
                v.wait_ge(v_steps, steps.up(1))
                tt(to[:, 2], rest[:], to[:, 1], ALU.subtract).then_inc(done.sem, 1)
                v.wait_ge(done.sem, done.of(b))

            def wide(x):
                return x[:].unsqueeze(2).to_broadcast([P, 2, NE])

            def narrow(x):
                return x.unsqueeze(1).to_broadcast([P, 2, NE])

            def choose(onehot, top):
                tt(r_a[:], lg[:], wide(top), ALU.is_equal).then_inc(v_steps, 1)
                v.wait_ge(v_steps, steps.up(1))
                v.scalar_tensor_tensor(out=r_b[:], in0=r_a[:], scalar=-2.0 * NE, in1=narrow(iota_e),
                                                       op0=ALU.mult, op1=ALU.add).then_inc(v_steps, 1)
                v.wait_ge(v_steps, steps.up(1))
                v.tensor_reduce(mv[:], r_b[:], AX.X, ALU.min).then_inc(v_steps, 1)
                v.wait_ge(v_steps, steps.up(1))
                tt(onehot[:], r_b[:], wide(mv), ALU.is_equal).then_inc(v_steps, 1)
                v.wait_ge(v_steps, steps.up(1))

            def step(s):
                y_, b, m, c, d, e = (s.batch(n) for n in ("y", "qk", "max", "out", "rec", "route"))
                row_max(m, 0)
                row_max(m, 1)
                if d.there:
                    v.wait_ge(a_f.sem, a_f.of(d))
                    v.wait_ge(a_i.sem, a_i.of(d))
                    if d.has(1):
                        v.wait_ge(g_gate.sem, g_gate.of(d.back(1)))
                    v.scalar_tensor_tensor(out=rc[:], in0=fg[:], scalar=EPS, in1=ig[:],
                                                           op0=ALU.add, op1=ALU.add).then_inc(v_steps, 1)
                    v.wait_ge(v_steps, steps.up(1))
                    v.reciprocal(rc[:, 0], rc[:, 0])
                row_max(m, 2)
                if d.there:
                    v.reciprocal(rc[:, 1], rc[:, 1]).then_inc(v_rc.sem, 1)
                row_max(m, 3)
                if c.there:
                    if c.has(1):
                        v.wait_ge(g_o.sem, g_o.of(c.back(1)))
                    for n in range(2):
                        v.wait_ge(pe_tr.sem, pe_tr.of(c, n + 1))
                        got = bank[f"tr{n}"][:].rearrange("p (h k) -> p h k", h=NH)
                        v.reciprocal(o_den[:, n], got[:, :, HD]).then_inc(v_steps, 1)
                        v.wait_ge(v_steps, steps.up(1))
                        tt(o_norm[:, n].rearrange("p (h k) -> p h k", h=NH), got[:, :, 0:HD],
                                       o_den[:, n].unsqueeze(2).to_broadcast([P, NH, HD]), ALU.mult).then_inc(v_tr.sem, 1)
                row_max(m, 4)
                row_max(m, 5)
                if e.there:
                    v.wait_ge(v_lg.sem, v_lg.of(e))
                    if e.has(1):
                        v.wait_ge(v_slot.sem, v_slot.of(e.back(1)))
                    v.tensor_reduce(m1[:], lg[:], AX.X, ALU.max).then_inc(v_steps, 1)
                    v.wait_ge(v_steps, steps.up(1))
                    choose(oh1, m1)
                    v.scalar_tensor_tensor(out=lg[:], in0=oh1[:], scalar=-1e30, in1=lg[:],
                                                           op0=ALU.mult, op1=ALU.add).then_inc(v_steps, 1)
                    v.wait_ge(v_steps, steps.up(1))
                    v.tensor_reduce(m2[:], lg[:], AX.X, ALU.max).then_inc(v_steps, 1)
                    v.wait_ge(v_steps, steps.up(1))
                    choose(oh2, m2)
                    tt(oh_b[:], oh1[:], oh2[:], ALU.add).then_inc(v_oh.sem, 1)
                    tt(ex[:], m2[:], m1[:], ALU.subtract).then_inc(v_dm.sem, 1)
                row_max(m, 6)
                row_max(m, 7)
                if b.there:
                    split(b, q_rope, q_split, g_q, q_stored, v_q)
                row_max(m, 8)
                if d.there:
                    v.wait_ge(pe["h"].sem, pe["h"].of(d))
                    v.wait_ge(g_gate.sem, g_gate.of(d))
                    if d.has(1):
                        v.wait_ge(v_hid.sem, v_hid.of(d.back(1)))
                    for k in range(2):
                        last = v.scalar_tensor_tensor(out=info[:, k], in0=bank["h"][:, k * NT:k * NT + NT],
                                                      scalar=bias[:, 5, k:k + 1], in1=ig[:, k],
                                                      op0=ALU.add, op1=ALU.mult)
                    last.then_inc(v_new.sem, 1)
                    v.wait_ge(a_ln.sem, a_ln.of(d))
                    if d.has(1):
                        v.wait_ge(a_dec.sem, a_dec.of(d.back(1)))
                    for k in range(2):
                        last = v.tensor_tensor_scan(lc[:, k, 1:NT + 1], ones_row[:], lr[:, k], 0.0, ALU.mult, ALU.add)
                    last.then_inc(v_cum.sem, 1)
                row_max(m, 9)
                if m.there:
                    v.wait_ge(pe["v"].sem, pe["v"].of(m))
                    if m.has(1):
                        v.wait_ge(g_v.sem, g_v.of(m.back(1)))
                    tt(v_lin[:].rearrange("p (c f) -> p c f", c=2),
                                  bank["v"][:].rearrange("p (c f) -> p c f", c=2),
                                  bv_sb[:].unsqueeze(1).to_broadcast([P, 2, D]), ALU.add).then_inc(v_v.sem, 1)
                row_max(m, 10)
                if b.there:
                    split(b, k_rope, k_split, g_k, k_stored, v_k)
                row_max(m, 11)
                if d.there:
                    v.wait_ge(a_dec.sem, a_dec.of(d))
                    v.wait_ge(v_new.sem, v_new.of(d))
                    tt(info[:], info[:], scaling[:], ALU.mult).then_inc(v_steps, 1)
                    v.wait_ge(v_steps, steps.up(1))
                    if d.has(1):
                        v.wait_ge(pe["lg"].sem, pe["lg"].of(d.back(1)))
                    for k in range(2):
                        v.tensor_tensor_scan(hid[:, k], ones_row[:], info[:, k], 0.0, ALU.mult, ALU.add).then_inc(v_steps, 1)
                    v.wait_ge(v_steps, steps.up(2))
                    for k in range(2):
                        last = v.scalar_tensor_tensor(out=hid[:, k], in0=decay[:, k],
                                                      scalar=cond_sb[:, k, bass.ds(d.index, 1)], in1=hid[:, k],
                                                      op0=ALU.mult, op1=ALU.add)
                    last.then_inc(v_hid.sem, 1)
                row_max(m, 12)
                if e.there:
                    v.wait_ge(pe["rank"].sem, pe["rank"].of(e))
                    tt(r_c[:], bank["rank"][:, 0:2 * NE].rearrange("p (c k) -> p c k", c=2),
                       narrow(at_e[:]), ALU.add).then_inc(v_steps, 1)
                    v.wait_ge(v_steps, steps.up(1))
                    tt(at_e[:], at_e[:], bank["rank"][:, 2 * NE:3 * NE], ALU.add).then_inc(v_rank.sem, 1)
                row_max(m, 13)
                if c.there:
                    v.wait_ge(pe["wo"].sem, pe["wo"].of(c))
                    v.wait_ge(res_loaded.sems[c.par], res_loaded.of(c))
                    if c.has(2):
                        v.wait_ge(pe["x1"].sem, pe["x1"].of(c.back(2)))
                    for k in range(2):
                        last = v.scalar_tensor_tensor(out=x1[:, c.par, k], in0=bank["wo"][:, k * NT:k * NT + NT],
                                                      scalar=bias[:, 2, k:k + 1], in1=x_res[:, k],
                                                      op0=ALU.add, op1=ALU.add)
                    last.then_inc(v_x1.sem, 1)
                row_max(m, 14)
                row_max(m, 15)
                if m.there:
                    v.wait_ge(v_max.sem, v_max.of(m))
                    if m.has(1):
                        v.wait_ge(pe["mt"].sem, pe["mt"].of(m.back(1)))
                    v.tensor_copy(mx_split[:, :, 0], mx[:]).then_inc(v_steps, 1)
                    v.wait_ge(v_steps, steps.up(1))
                    tt(mx_split[:, :, 1], mx[:], mx_split[:, :, 0], ALU.subtract).then_inc(v_mx.sem, 1)
                if y_.there:
                    v.wait_ge(x_loaded.sems[y_.par], x_loaded.of(y_))
                    if y_.has(2):
                        v.wait_ge(pe["v"].sem, pe["v"].of(y_.back(2)))
                    for k in range(2):
                        last = v.tensor_scalar(y[:, y_.par, k], x_in[:, k], g1[:, k, bass.ds(y_.index, 1)],
                                               None, ALU.mult)
                    last.then_inc(v_y.sem, 1)
                if m.there:
                    v.wait_ge(pe["mt"].sem, pe["mt"].of(m))
                    if m.has(1):
                        v.wait_ge(max_loaded.sems[m.back(1).par], max_loaded.of(m.back(1)))
                    v.tensor_copy(mx_rows[:], bank["mt"][0:2 * NH, 0:NT // 2].bitcast(BF16)).then_inc(v_mt.sem, 1)
                if d.there:
                    v.wait_ge(pe["lg"].sem, pe["lg"].of(d))
                    if d.has(1):
                        v.wait_ge(v_oh.sem, v_oh.of(d.back(1)))
                    v.tensor_copy(lg[:].rearrange("p c k -> p (c k)"), bank["lg"][:, 0:2 * NE]).then_inc(v_lg.sem, 1)
                if e.there:
                    if e.has(1):
                        v.wait_ge(scattered.sems[e.back(1).par], scattered.of(e.back(1)))
                    v.wait_ge(a_re.sem, a_re.of(e))
                    tt(r_a[:], r_c[:], oh1[:], ALU.mult).then_inc(v_steps, 1)
                    steps.up(1)
                    tt(r_b[:], r_c[:], oh2[:], ALU.mult).then_inc(v_steps, 1)
                    v.wait_ge(v_steps, steps.up(1))
                    v.tensor_reduce(sl[:, 0], r_a[:], AX.X, ALU.add).then_inc(v_steps, 1)
                    steps.up(1)
                    v.tensor_reduce(sl[:, 1], r_b[:], AX.X, ALU.add).then_inc(v_steps, 1)
                    v.wait_ge(v_steps, steps.up(1))
                    v.tensor_copy(slots[:], sl[:]).then_inc(v_steps, 1)
                    steps.up(1)
                    v.tensor_scalar(w1c[:], ex[:], 1.0, None, ALU.add).then_inc(v_steps, 1)
                    v.wait_ge(v_steps, steps.up(1))
                    v.reciprocal(w1c[:], w1c[:]).then_inc(v_steps, 1)
                    v.wait_ge(v_steps, steps.up(1))
                    tt(w2c[:], ex[:], w1c[:], ALU.mult).then_inc(v_steps, 1)
                    v.wait_ge(v_steps, steps.up(1))
                    tt(oh1[:], oh1[:], wide(w1c), ALU.mult).then_inc(v_steps, 1)
                    steps.up(1)
                    tt(oh2[:], oh2[:], wide(w2c), ALU.mult).then_inc(v_steps, 1)
                    v.wait_ge(v_steps, steps.up(1))
                    tt(hrow[:, e.par, :, ROW_W:ROW_W + NE], oh1[:], oh2[:], ALU.add).then_inc(v_steps, 1)
                    steps.up(1)
                    v.tensor_copy(hrow[:, e.par, :, ROW_ID:ROW_ID + 1].bitcast(U32),
                                                  tid[:].unsqueeze(2)).then_inc(v_steps, 1)
                    v.wait_ge(v_steps, steps.up(1))
                    v.tensor_scalar(tid[:], tid[:], float(NT), None, ALU.add).then_inc(v_slot.sem, 1)

            all_steps(v, step, [(steps, V_STEPS * UNROLL)])

            v.wait_ge(v_rank.sem, v_rank.of(Batch(None, NB - 1)))
            tt(cnt[:], at_e[:], region_e, ALU.subtract).then_inc(v_steps, 1)
            v.wait_ge(v_steps, steps.up(1))
            v.tensor_scalar(cnt[:], cnt[:], float(P - 1), None, ALU.add).then_inc(v_steps, 1)
            v.wait_ge(v_steps, steps.up(1))
            v.tensor_copy(cnt_i[:], cnt[:]).then_inc(v_steps, 1)
            v.wait_ge(v_steps, steps.up(1))
            v.tensor_scalar(cnt_i[:], cnt_i[:], P.bit_length() - 1, None, ALU.logical_shift_right).then_inc(v_steps, 1)
            v.wait_ge(v_steps, steps.up(1))
            v.tensor_copy(nblk[:], cnt_i[:]).then_inc(v_steps, 1)
            v.wait_ge(v_steps, steps.up(1))
            v.tensor_copy(at_i[:], at_e[:]).then_inc(v_steps, 1)
            steps.up(1)
            v.tensor_tensor_scan(endb[:], ones_row[:, 0:NE], nblk[:], 0.0, ALU.mult, ALU.add).then_inc(v_steps, 1)
            v.wait_ge(v_steps, steps.up(1))

            def by_block(x):
                return x.unsqueeze(1).to_broadcast([P, NBLK, NE])

            def by_expert(x):
                return x.unsqueeze(2).to_broadcast([P, NBLK, NE])

            tt(blk_ge[:], by_expert(blk[:]), by_block(endb[:]), ALU.is_ge).then_inc(v_steps, 1)
            v.wait_ge(v_steps, steps.up(1))
            v.tensor_reduce(blk_e[:], blk_ge[:], AX.X, ALU.add).then_inc(v_steps, 1)
            v.wait_ge(v_steps, steps.up(1))
            tt(blk_oh[:], by_expert(blk_e[:]), by_block(iota_e), ALU.is_equal).then_inc(v_steps, 1)
            steps.up(1)
            tt(blk_ge[:], blk_ge[:], by_block(nblk[:]), ALU.mult).then_inc(v_steps, 1)
            v.wait_ge(v_steps, steps.up(1))
            v.tensor_reduce(blk_s[:], blk_ge[:], AX.X, ALU.add).then_inc(v_steps, 1)
            v.wait_ge(v_steps, steps.up(1))
            tt(blk_s[:], blk[:], blk_s[:], ALU.subtract).then_inc(v_steps, 1)
            v.wait_ge(v_steps, steps.up(1))
            v.tensor_scalar(blk_s[:], blk_s[:], float(P), None, ALU.mult).then_inc(v_steps, 1)
            v.wait_ge(v_steps, steps.up(1))
            v.scalar_tensor_tensor(out=blk_s[:], in0=blk_e[:], scalar=float(REGION), in1=blk_s[:],
                                                   op0=ALU.mult, op1=ALU.add).then_inc(v_steps, 1)
            v.wait_ge(v_steps, steps.up(1))
            v.tensor_scalar(row_tab[:], blk_s[:], float(PAD_ROW), None, ALU.min).then_inc(v_steps, 1)
            steps.up(1)
            v.tensor_scalar(exp_tab[:], blk_e[:], float(NE - 1), float(2 * FF), ALU.min, ALU.mult).then_inc(tables_ready, 1)

            def ffn(n_x, n_g, n_d):
                if n_x.there:
                    v.wait_ge(f_tx.sem, f_tx.of(n_x))
                    if n_x.has(2):
                        v.wait_ge(f_u.sem, f_u.of(n_x.back(2)))
                    v.tensor_copy(xb_T[:, n_x.par % 2].rearrange("p c t -> p (c t)"), ps_tx[:, 0:2 * P]).then_inc(f_xT.sem, 1)
                if n_d.there:
                    v.wait_ge(xb_in.sems[n_d.par], xb_in.of(n_d))
                    if n_d.has(1):
                        v.wait_ge(f_out.sem, f_out.of(n_d.back(1)))
                    tt(wsel[:], xb[:, n_d.par, ROW_W:ROW_W + NE],
                       blk_oh[:, bass.ds(n_d.index, 1), :].rearrange("p o e -> p (o e)"), ALU.mult).then_inc(f_w, 1)
                    v.wait_ge(f_w, n_d.index * 2 + 1)
                    v.tensor_reduce(wrow[:, 0:1], wsel[:], AX.X, ALU.add).then_inc(f_w, 1)
                    v.wait_ge(f_w, n_d.index * 2 + 2)
                    v.wait_ge(f_y.sem, f_y.of(n_d))
                    if n_d.has(2):
                        v.wait_ge(added.sems[n_d.back(2).par], added.of(n_d.back(2)))
                    v.tensor_scalar(ysb[:, n_d.par % 2], ps_y[n_d.par % 2][:, 0:D], wrow[:, 0:1],
                                                 None, ALU.mult).then_inc(f_out.sem, 1)
                if n_g.there:
                    v.wait_ge(f_silu.sem, f_silu.of(n_g))
                    v.wait_ge(f_u.sem, f_u.of(n_g))
                    if n_g.has(2):
                        v.wait_ge(f_tg.sem, f_tg.of(n_g.back(2)))
                    tt(gu[:, n_g.par % 2], silu[:, n_g.par % 2], ps_u[n_g.par % 2], ALU.mult).then_inc(f_gu.sem, 1)

            v.wait_ge(tables_ready, 1)
            ffn_steps(v, ffn, 0, 1, 2)

        @block.tensor
        def _(pe_):
            pe_.wait_ge(consts_in, CONSTS)
            for stage, (w, x) in enumerate(((w1_sb, cond_sb), (w2_sb, gh))):
                if stage:
                    pe_.wait_ge(gate_v, 5)
                for c in range(2):
                    for k in range(2):
                        last = pe_.matmul(ps_job[stage][:, c * NB:c * NB + NB], w[:, k, c * P:c * P + P], x[:, k],
                                          start=(k == 0), stop=(k == 1))
                last.then_inc(gate_pe, 1)
            pe_.wait_ge(setup_done, SETUP_DONE)
            pe_.wait_ge(gate_v, 5)

            def project(s, name, stage, w, x):
                b = s.batch(stage)
                if b.there:
                    for free, value in bank_free(s, name):
                        pe_.wait_ge(free, value)
                    for c in range(2):
                        for k in range(2):
                            last = pe_.matmul(bank[name][:, c * NT:c * NT + NT], w[:, k, c * P:c * P + P], x(b)[:, k],
                                              start=(k == 0), stop=(k == 1))
                    last.then_inc(pe[name].sem, 1)

            def turn(s, name, stage, x):
                b = s.batch(stage)
                if b.there:
                    for free, value in bank_free(s, name):
                        pe_.wait_ge(free, value)
                    for i in range(2):
                        for j in range(2):
                            last = pe_.transpose(bank[name][:, i * 256 + j * P:i * 256 + j * P + P],
                                                 x(b)[:, j, i * P:i * P + P], ident)
                    last.then_inc(pe[name].sem, 1)

            def outputs(s, g, stage):
                b = s.batch(stage)
                if b.there:
                    pe_.wait_ge(a_exp.sem, a_exp.of(b, 2 * g + 2))
                    if g == 0:
                        pe_.wait_ge(g_v.sem, g_v.of(b))
                    for free, value in bank_free(s, f"pv{g}"):
                        pe_.wait_ge(free, value)
                    for k in range(2):
                        for j in range(4):
                            h = 4 * g + j
                            last = pe_.matmul(bank[f"pv{g}"][32 * j:32 * j + 32, 0:NT], v_aug[:, b.par, NH * k + h],
                                              probs[:, h % 8, k], start=(k == 0), stop=(k == 1))
                    last.then_inc(pe_pv.sem, 1)

            def scores(s, u):
                b = s.batch("att")
                if b.there:
                    if u == 0:
                        pe_.wait_ge(max_loaded.sems[b.par], max_loaded.of(b))
                    if u >= 2:
                        pe_.wait_ge(a_exp.sem, a_exp.of(b, u - 1))
                    else:
                        if b.has(1):
                            pe_.wait_ge(a_exp.sem, a_exp.of(b.back(1), 7 + u))
                    for n in range(2):
                        h = 2 * u + n
                        for k in range(2):
                            last = pe_.matmul(ps_st[u % 2][:, n, k], k_rows[0:SCORE_ROWS, b.par, h, k * P:k * P + P],
                                              q_rows[0:SCORE_ROWS, b.par, h], start=True, stop=True)
                    last.then_inc(pe_st.sem, 1)

            def max_scores(s, h):
                b = s.batch("max")
                if b.there:
                    if h == 0:
                        pe_.wait_ge(rows_loaded.sems[b.par], rows_loaded.of(b))
                    if h >= 2:
                        pe_.wait_ge(v_max.sem, v_max.of(b, h - 1))
                    else:
                        if b.has(1):
                            pe_.wait_ge(v_max.sem, v_max.of(b.back(1), NH - 1 + h))
                    for c in range(2):
                        last = pe_.matmul(ps_sm[h % 2][:, c], q_rows[0:SPLIT_ROWS, b.par, h, c * P:c * P + P],
                                          k_rows[0:SPLIT_ROWS, b.par, h], start=True, stop=True)
                    last.then_inc(pe_sm.sem, 1)

            def turn_outputs(s):
                c = s.batch("out")
                if c.there:
                    pe_.wait_ge(a_ov.sem, a_ov.of(c))
                    for n in range(2):
                        for free, value in bank_free(s, f"tr{n}"):
                            pe_.wait_ge(free, value)
                        for g in range(4):
                            last = pe_.transpose(bank[f"tr{n}"][:, g * P:g * P + P], o_raw[:, g, n * P:n * P + P], ident)
                        last.then_inc(pe_tr.sem, 1)

            def values(s):
                m = s.batch("max")
                if m.there:
                    pe_.wait_ge(v_y.sem, v_y.of(m))
                    for free, value in bank_free(s, "v"):
                        pe_.wait_ge(free, value)
                    for c in range(2):
                        for k in range(2):
                            last = pe_.matmul(bank["v"][:, c * D:c * D + D], y[:, m.par, k, c * P:c * P + P], wv[:, k],
                                              start=(k == 0), stop=(k == 1))
                    last.then_inc(pe["v"].sem, 1)

            def ranks(s):
                e = s.batch("route")
                if e.there:
                    pe_.wait_ge(v_oh.sem, v_oh.of(e))
                    for free, value in bank_free(s, "rank"):
                        pe_.wait_ge(free, value)
                    rank = bank["rank"]
                    pe_.matmul(rank[:, 0:NE], upper, oh_b[:, 0], start=True, stop=True)
                    pe_.matmul(rank[:, NE:2 * NE], upper, oh_b[:, 1], start=True, stop=False)
                    pe_.matmul(rank[:, NE:2 * NE], ones, oh_b[:, 0], start=False, stop=True)
                    pe_.matmul(rank[:, 2 * NE:3 * NE], ones, oh_b[:, 0], start=True, stop=False)
                    pe_.matmul(rank[:, 2 * NE:3 * NE], ones, oh_b[:, 1], start=False, stop=True).then_inc(pe["rank"].sem, 1)

            def turn_maxima(s):
                m = s.batch("max")
                if m.there:
                    pe_.wait_ge(v_mx.sem, v_mx.of(m))
                    for free, value in bank_free(s, "mt"):
                        pe_.wait_ge(free, value)
                    for c in range(2):
                        last = pe_.transpose(bank["mt"][0:2 * NH, c * P // 2:c * P // 2 + P // 2].bitcast(BF16),
                                             mx_split[:, c].rearrange("p a h -> p (a h)"), ident_b[:])
                    last.then_inc(pe["mt"].sem, 1)

            def logits(s):
                d = s.batch("rec")
                if d.there:
                    for free, value in bank_free(s, "lg"):
                        pe_.wait_ge(free, value)
                    for c in range(2):
                        for k in range(2):
                            last = pe_.matmul(bank["lg"][:, c * NE:c * NE + NE], hid[:, k, c * P:c * P + P], gw[:, k],
                                              start=(k == 0), stop=(k == 1))
                    last.then_inc(pe["lg"].sem, 1)

            def step(s):
                b, c, d = (s.batch(n) for n in ("qk", "out", "rec"))
                x1_of, y_of = (lambda z: x1[:, z.par]), (lambda z: y[:, z.par])
                if d.there:
                    pe_.wait_ge(v_x1.sem, v_x1.of(d))
                project(s, "f", "rec", wf, x1_of)
                max_scores(s, 0)
                project(s, "i", "rec", wi, x1_of)
                max_scores(s, 1)
                if b.there:
                    pe_.wait_ge(v_y.sem, v_y.of(b))
                project(s, "q", "qk", wq, y_of)
                max_scores(s, 2)
                scores(s, 0)
                outputs(s, 3, "out")
                max_scores(s, 3)
                turn_outputs(s)
                max_scores(s, 4)
                scores(s, 1)
                project(s, "k", "qk", wk, y_of)
                max_scores(s, 5)
                scores(s, 2)
                max_scores(s, 6)
                outputs(s, 0, "att")
                max_scores(s, 7)
                project(s, "h", "rec", wh, x1_of)
                max_scores(s, 8)
                scores(s, 3)
                values(s)
                max_scores(s, 9)
                scores(s, 4)
                max_scores(s, 10)
                outputs(s, 1, "att")
                max_scores(s, 11)
                if c.there:
                    pe_.wait_ge(g_o.sem, g_o.of(c))
                turn(s, "aro", "out", lambda z: o_rope)
                scores(s, 5)
                max_scores(s, 12)
                ranks(s)
                if c.there:
                    pe_.wait_ge(a_at.sem, a_at.of(c))
                project(s, "wo", "out", wo, lambda z: o_T)
                max_scores(s, 13)
                scores(s, 6)
                max_scores(s, 14)
                turn(s, "x1", "rec", x1_of)
                max_scores(s, 15)
                outputs(s, 2, "att")
                scores(s, 7)
                turn_maxima(s)
                if d.there:
                    pe_.wait_ge(v_hid.sem, v_hid.of(d))
                turn(s, "hid", "rec", lambda z: hid)
                logits(s)

            all_steps(pe_, step)

            pe_.wait_ge(experts_in, 48)
            pe_.wait_ge(tables_ready, 1)

            def ffn(n_x, n_g, n_d):
                if n_g.there:
                    at = pe_.value_load(exp_tab[0:1, bass.ds(n_g.index, 1)], min_val=0, max_val=(NE - 1) * 2 * FF)
                    pe_.wait_ge(f_xT.sem, f_xT.of(n_g))
                    if n_g.has(2):
                        pe_.wait_ge(f_silu.sem, f_silu.of(n_g.back(2)))
                    if n_g.has(2):
                        pe_.wait_ge(f_gu.sem, f_gu.of(n_g.back(2)))
                    for k in range(2):
                        last = pe_.matmul(ps_g[n_g.par % 2], xb_T[:, n_g.par % 2, k],
                                          wg_all[:, bass.ds(at + k * FF, FF)], start=(k == 0), stop=(k == 1))
                    last.then_inc(f_g.sem, 1)
                if n_d.there:
                    pe_.wait_ge(f_gu.sem, f_gu.of(n_d))
                    if n_d.has(1):
                        pe_.wait_ge(f_guT.sem, f_guT.of(n_d.back(1)))
                    for k in range(4):
                        last = pe_.transpose(ps_tg[:, k * P:k * P + P], gu[:, n_d.par % 2, k * P:k * P + P], ident)
                    last.then_inc(f_tg.sem, 1)
                if n_g.there:
                    for k in range(2):
                        last = pe_.matmul(ps_u[n_g.par % 2], xb_T[:, n_g.par % 2, k],
                                          wu_all[:, bass.ds(at + k * FF, FF)], start=(k == 0), stop=(k == 1))
                    last.then_inc(f_u.sem, 1)
                if n_x.there:
                    pe_.wait_ge(xb_in.sems[n_x.par], xb_in.of(n_x))
                    if n_x.has(1):
                        pe_.wait_ge(f_xT.sem, f_xT.of(n_x.back(1)))
                    for k in range(2):
                        last = pe_.transpose(ps_tx[:, k * P:k * P + P], xb[:, n_x.par, k * P:k * P + P], ident)
                    last.then_inc(f_tx.sem, 1)
                if n_d.there:
                    at = pe_.value_load(exp_tab[0:1, bass.ds(n_d.index, 1)], min_val=0, max_val=(NE - 1) * 2 * FF)
                    pe_.wait_ge(f_guT.sem, f_guT.of(n_d))
                    if n_d.has(2):
                        pe_.wait_ge(f_out.sem, f_out.of(n_d.back(2)))
                    for k in range(4):
                        last = pe_.matmul(ps_y[n_d.par % 2][:, 0:D], gu_T[:, k], wd_all[:, bass.ds(at + k * D, D)],
                                          start=(k == 0), stop=(k == 3))
                    last.then_inc(f_y.sem, 1)

            ffn_steps(pe_, ffn, 0, 1, 2)


def by_partition(a):
    return np.ascontiguousarray(a.reshape(-1, P, a.shape[-1]).transpose(1, 0, 2))


def kernel(**inputs):
    import concourse.bacc as bacc
    from concourse.bass_utils import run_bass_kernel_spmd

    a = {n: np.asarray(v) for n, v in inputs.items()}
    def qk_order(w):
        return w.reshape(NH, HALF, 2, -1).transpose(2, 1, 0, 3).reshape(D, -1)

    def v_order(w):
        return w.reshape(NH, HALF, 2, -1).transpose(2, 0, 1, 3).reshape(D, -1)

    def weight(w):
        return by_partition(w.T)

    def column(b):
        return np.ascontiguousarray(b.reshape(2, P).T)

    cos, sin = rope_tables()
    cs = np.stack([cos, sin])
    by_pair = np.repeat(cs.transpose(0, 2, 1), NH, axis=1)
    rope_qk = np.stack([by_pair, by_pair[::-1]]).transpose(2, 0, 1, 3).reshape(P, -1)
    v_tab = np.tile(cs.transpose(1, 0, 2).reshape(2, P, 2, 1, HALF), (1, 1, 1, NH, 1))
    rope_v = np.stack([v_tab, v_tab[:, :, ::-1]]).transpose(2, 0, 1, 3, 4, 5).reshape(P, -1)
    o_tab = np.stack([np.stack([-cos, sin], -1), np.stack([-sin, -cos], -1)])
    o_tab = np.tile(o_tab.reshape(2, 2, P, 1, HD), (1, 1, 1, NH, 1))
    rope_out = o_tab.transpose(2, 0, 1, 3, 4).reshape(P, -1)
    const = np.zeros((P, 3 * P + 64), np.float32)
    const[:, 0:P] = np.eye(P)
    const[:, P:2 * P] = np.triu(np.ones((P, P)), 1)
    const[:, 2 * P:3 * P] = 1.0
    const[:, 3 * P:3 * P + NE] = np.arange(NE)
    const[:, 3 * P + NE:3 * P + 2 * NE] = np.arange(NE) * REGION
    const[:, 3 * P + 2 * NE:3 * P + 2 * NE + 2] = np.arange(P)[:, None] + np.array([0, P])[None, :]

    arrays = {
        "xT": a["x"].transpose(2, 0, 1),
        "condT": by_partition(a["cond_1024"].T),
        "w1T": weight(a["L0_cond_W1"]), "b1": column(a["L0_cond_b1"]),
        "w2T": weight(a["L0_cond_W2"]), "b2": column(a["L0_cond_b2"]),
        "wqT": weight(qk_order(a["L0_attn_Wq"])), "bq": column(qk_order(a["L0_attn_bq"])),
        "wkT": weight(qk_order(a["L0_attn_Wk"])), "bk": column(qk_order(a["L0_attn_bk"])),
        "wvT": weight(v_order(a["L0_attn_Wv"])),
        "bv": np.broadcast_to(v_order(a["L0_attn_bv"]).reshape(1, D), (P, D)),
        "woT": weight(a["L0_attn_Wo"]), "bo": column(a["L0_attn_bo"]),
        "wfT": weight(a["L0_cond2_W_f"]), "bf": column(a["L0_cond2_b_f"]),
        "wiT": weight(a["L0_cond2_W_i"]), "bi": column(a["L0_cond2_b_i"]),
        "whT": weight(a["L0_cond2_W_h"]), "bh": column(a["L0_cond2_b_h"]),
        "gate_w": by_partition(a["L0_ffn_gate_w"]),
        "w_gate": a["L0_ffn_gate_proj_w"].reshape(NE, 2, P, FF).transpose(2, 0, 1, 3).reshape(P, -1),
        "w_up": a["L0_ffn_up_proj_w"].reshape(NE, 2, P, FF).transpose(2, 0, 1, 3).reshape(P, -1),
        "w_down": a["L0_ffn_down_proj_w"].reshape(NE, 4, P, D).transpose(2, 0, 1, 3).reshape(P, -1),
        "rope_qk": rope_qk, "rope_v": rope_v, "rope_out": rope_out, "constants": const,
        "block_numbers": np.broadcast_to(np.arange(NBLK, dtype=np.float32)[None, :], (P, NBLK)),
    }
    arrays = {f"in_{n}": np.ascontiguousarray(v) for n, v in arrays.items()}
    nc = bacc.Bacc("TRN2", target_bir_lowering=False, num_devices=1)
    args = {n[3:]: nc.dram_tensor(n, v.shape, mybir.dt.from_np(v.dtype), kind="ExternalInput").ap()
            for n, v in arrays.items()}
    out = nc.dram_tensor("out_rows", (TOKENS + P, D), F32, kind="ExternalOutput").ap()
    build(nc, out=out, **args)
    result = run_bass_kernel_spmd(nc, [arrays], core_ids=[0]).results[0]["out_rows"]
    return result[:TOKENS].reshape(NB, NT, D)
```

```python
from contextlib import ExitStack

import numpy as np

import concourse.bass as bass
from concourse import mybir

F32 = mybir.dt.float32
BF16 = mybir.dt.bfloat16
F32R = mybir.dt.float32r
I32 = mybir.dt.int32
U32 = mybir.dt.uint32
ALU = mybir.AluOpType
ACT = mybir.ActivationFunctionType
AX = mybir.AxisListType

P = 128
NB, NT, D = 32, 256, 256
NH, HD = 16, 16
HALF = HD // 2
NE, FF = 8, 512
TOKENS = NB * NT
EPS = 1e-8
SCALE = 1.0 / HD ** 0.5

SPLIT_ROWS = 6 * HD
SCORE_ROWS = SPLIT_ROWS + 2

ROW = 272
ROW_W, ROW_ID = D, D + NE
REGION = TOKENS + P
PAD_ROW = NE * REGION
SORTED = PAD_ROW + P
XBUF = 4
BLOCKS = 2 * TOKENS // P + NE - 1

NBLK = -(-BLOCKS // XBUF) * XBUF

SMALL_SIZES = {"bias": 16, "gate_w": 2 * NE, "cond": 2 * NB, "bv": D, "blocks": NBLK, "ident": P, "upper": P,
               "ones": P, "iota_e": NE, "region_e": NE, "token_p": 2}
SMALL = sum(SMALL_SIZES.values())
SMALL_AT = {name: (sum(list(SMALL_SIZES.values())[:n]), size) for n, (name, size) in enumerate(SMALL_SIZES.items())}

LATE_WORDS = XBUF * ROW + 4 * D + 4 * FF + NBLK * NE
MID_WORDS = NE * 2 * FF + LATE_WORDS
PARTS = 4

STAGES = {"y": 0, "qk": 1, "max": 2, "att": 3, "out": 4, "rec": 5, "route": 6}
DEPTH = max(STAGES.values())
STEPS = NB + DEPTH
LOOP_FROM, LOOP_TO = DEPTH + 2, NB
UNROLL = 2
N_IN_LOOP = (LOOP_TO - LOOP_FROM) // UNROLL

V_STEPS = 37

JOBS = [("f", "rec"), ("i", "rec"), ("q", "qk"), ("pv3", "out"), ("tr0", "out"), ("tr1", "out"),
        ("k", "qk"), ("pv0", "att"), ("h", "rec"), ("v", "max"), ("aro", "out"), ("pv1", "att"),
        ("pv2", "att"), ("rank", "route"), ("wo", "out"), ("x1", "rec"), (None, None), ("hid", "rec"),
        ("lg", "rec"), ("mt", "max")]


class Batch:

    def __init__(self, i, offset, count=NB, cycle=UNROLL):
        self.par, self.index, self.turn = offset % cycle, offset, offset // cycle
        if i is not None:
            self.index, self.turn = i * cycle + offset, i + offset // cycle
        self.i, self.offset, self.count, self.cycle = i, offset, count, cycle

    def back(self, n):
        return Batch(self.i, self.offset - n, self.count, self.cycle)

    @property
    def there(self):
        return self.i is not None or 0 <= self.offset < self.count

    def has(self, n):
        return self.i is not None or self.offset >= n


class Step:

    def __init__(self, i, offset):
        self.i, self.offset = i, offset

    def batch(self, stage, before=0):
        return Batch(self.i, self.offset - before - STAGES[stage])


class Event:

    def __init__(self, sem, per=1):
        self.sem, self.per = sem, per

    def of(self, batch, k=None):
        return batch.index * self.per + (self.per if k is None else k)


class Transfer:

    def __init__(self, sems, per=1):
        self.sems, self.per = sems, per

    def of(self, batch):
        return (batch.turn + 1) * (16 * self.per)


class Count:

    def __init__(self):
        self.base, self.n, self.i, self.per = 0, 0, None, 0

    def enter(self, i, per):
        self.base, self.n, self.i, self.per = self.base + self.n, 0, i, per

    def leave(self, times):
        assert self.n == self.per, (self.n, self.per)
        self.base, self.n, self.i = self.base + self.per * times, 0, None

    def up(self, n):
        self.n += n
        value = self.base + self.n
        return value if self.i is None else self.i * self.per + value


def rope_tables():
    position = np.arange(NT, dtype=np.float32)[:, None]
    pair = np.arange(0, HD, 2, dtype=np.float32)[None, :]
    freqs = position * (np.float32(10000.0) ** (-pair / np.float32(HD)))
    rope = np.concatenate([np.cos(freqs), np.sin(freqs)], axis=-1).astype(np.float32)
    return rope[:, ::2], rope[:, 1::2]


def build(nc, xT, gate_weights, small, early_weights, late_weights, rope_tokens, w_gate, w_up, w_down, out):
    with ExitStack() as ctx:
        def sb(name, shape, dt=F32):
            return ctx.enter_context(nc.sbuf_tensor(name, shape, dt))

        def sem(name):
            return ctx.enter_context(nc.semaphore(name))

        def event(name, per=1):
            return Event(sem(name), per)

        def transfer(name, per=1, cycle=UNROLL):
            return Transfer([sem(f"{name}{p}") for p in range(cycle)], per)

        q_parts = nc.dram_tensor("q_parts", (6, P, NT), BF16).ap()
        k_parts = nc.dram_tensor("k_parts", (6, P, NT), BF16).ap()
        sorted_rows = nc.dram_tensor("sorted_rows", (SORTED, ROW), F32).ap()

        with ExitStack() as pipeline:
            def sb_early(name, words):
                return pipeline.enter_context(nc.sbuf_tensor(name, [P, words], F32))

            gate_mem = sb_early("gate_mem", NE * 2 * FF)
            stage_mem = sb_early("stage_mem", NE * 2 * FF)
            scores_mem = sb_early("scores_mem", NE * 4 * D)
            att_mem = sb_early("att_mem", 18 * 2 * NT)
            mid_mem = sb_early("mid_mem", MID_WORDS)
        wg_high, wu_high = sb("wg_high", [P, NE * 2 * FF], F32R), sb("wu_high", [P, NE * 2 * FF], F32R)
        wd_all = sb("wd_all", [P, NE * 4 * D])
        wg_low = sb("wg_low", [P, NE * 2 * FF], F32R)
        gu_T, ysb = sb("gu_T", [P, 4, P]), sb("ysb", [P, 2, D])
        wu_low = sb("wu_low", [P, NE * 2 * FF], F32R)
        xb_T = sb("xb_T", [P, 2, 2, 2, P], F32R)
        xb = sb("xb", [P, XBUF, ROW])
        silu, gu = sb("silu", [P, 2, FF]), sb("gu", [P, 2, FF])
        blk_oh = sb("blk_oh", [P, NBLK, NE])

        def over(mem):
            used = [0]

            def cut(shape, dt=F32):
                n = int(np.prod(shape))
                words = n if dt != BF16 else n // 2
                view = mem[:, used[0]:used[0] + words]
                used[0] += words
                assert used[0] <= mem.shape[1], (used[0], mem.shape)
                view = view if dt == F32 else view.bitcast(dt)
                names = "abcd"[:len(shape)]
                return view.rearrange(f"p ({' '.join(names)}) -> p {' '.join(names)}", **dict(zip(names, shape)))
            return cut

        small_sb = sb("small_sb", [P, SMALL])

        def small_view(name, shape=None):
            at, n = SMALL_AT[name]
            view = small_sb[:, at:at + n]
            return view if shape is None else view.rearrange("p (a b) -> p a b", a=shape[0], b=shape[1])
        middle = over(mid_mem)
        late_w = middle([4, 2, D])
        wo, wf, wi, wh = (late_w[:, n] for n in range(4))
        rope_tok = middle([2, 2, 2 * D])
        rv = rope_tok[:, 0]
        ro = rope_tok[:, 1]
        bias = small_view("bias", [8, 2])
        gw, cond_sb = small_view("gate_w", [2, NE]), small_view("cond", [2, NB])
        bv_sb, blk = small_view("bv"), small_view("blocks")
        ident, upper, ones = small_view("ident"), small_view("upper"), small_view("ones")
        iota_e, region_e, token_p = small_view("iota_e"), small_view("region_e"), small_view("token_p")
        ident_b = sb("ident_b", [P, P], BF16)
        counters = sb("counters", [P, 2 * P], BF16)
        g1 = sb("g1", [P, 2, NB])
        gh = sb("gh", [P, 2, NB])
        gs = sb("gs", [P, 2, NB])
        ones_row = sb("ones_row", [P, NT])
        eps_sb = sb("eps_sb", [P, 1])

        early = over(stage_mem)
        wq, wk, wv = early([2, D]), early([2, D]), early([2, D])
        rqk = early([2, 2 * NT])
        EARLY_WEIGHTS = 3 * 2 * D + 2 * 2 * NT
        x_in = early([2, NT])
        x_res = middle([2, NT])
        y = early([2, 2, NT])
        q_lin, k_lin = early([2 * NT]), early([2 * NT])
        t1, t2 = middle([2 * NT]), middle([2 * NT])
        q_rope, k_rope = early([2 * NT]), early([2 * NT])
        q_split, k_split = early([3, 2 * NT], BF16), early([3, 2 * NT], BF16)
        rest = early([2 * NT])
        operands = over(scores_mem)
        q_rows, k_rows = operands([2, NH, NT], BF16), operands([2, NH, NT], BF16)
        attention = over(att_mem)
        probs = attention([8, 2, NT])
        v_aug = attention([2, 2 * NH, 2 * HD])
        v_lin = attention([2 * D])
        mx = sb("mx", [P, 2, NH])
        mx_split = sb("mx_split", [P, 2, 2, NH], BF16)
        mx_rows = sb("mx_rows", [2 * NH, NT], BF16)
        o_raw = attention([4, NT])
        o_den = sb("o_den", [P, 2, NH])
        o_norm, o_rope, o_T = attention([2, D]), attention([2, D]), attention([2, NT])
        x1 = middle([2, 2, NT])
        x1_row = middle([2, D])
        fg, ig = middle([2, NT]), middle([2, NT])
        rc = middle([2, NT])
        lr = middle([2, NT])
        lc = middle([2, NT + 1])
        scaling = middle([2, NT])
        decay = middle([2, NT])
        info = middle([2, NT])
        hid = middle([2, NT])
        hrow = sb("hrow", [P, 2, 2, ROW])
        lg = sb("lg", [P, 2, NE])
        r_a, r_b, r_c, oh1, oh2 = (sb(n, [P, 2, NE]) for n in ("r_a", "r_b", "r_c", "oh1", "oh2"))
        m1, m2, mv, ex, w1c, w2c = (sb(n, [P, 2]) for n in ("m1", "m2", "mv", "ex", "w1c", "w2c"))
        sl = sb("sl", [P, 2, 2])
        oh_b = sb("oh_b", [P, 2, NE], BF16)
        slots = sb("slots", [P, 2, 2, 2], U32)
        tid = sb("tid", [P, 2])
        at_e = sb("at_e", [P, NE])

        ps_st = [ctx.enter_context(nc.psum_tensor(f"ps_st{i}", [P, 2, 2, NT], F32)) for i in range(2)]
        ps_sm = [ctx.enter_context(nc.psum_tensor(f"ps_sm{i}", [P, 2, NT], F32)) for i in range(2)]
        ps_job = [ctx.enter_context(nc.psum_tensor(f"ps_job{i}", [P, 512], F32)) for i in range(2)]
        bank = {name: ps_job[n % 2] for n, (name, _) in enumerate(JOBS)}

        gate_in, consts_in = sem("gate_in"), sem("consts_in")
        setup_done = sem("setup_done")
        gate_w_in, up_w_in, down_w_in = sem("gate_w_in"), sem("up_w_in"), sem("down_w_in")
        low_begun, high_made = sem("low_begun"), sem("high_made")
        low_by_pool, low_by_vector = sem("low_by_pool"), sem("low_by_vector")
        gate_pe, gate_act, gate_v = sem("gate_pe"), sem("gate_act"), sem("gate_v")
        x_loaded, res_loaded = transfer("x_loaded"), transfer("res_loaded")
        q_stored, k_stored = transfer("q_stored"), transfer("k_stored")
        rows_loaded = transfer("rows_loaded", 9)
        max_loaded = transfer("max_loaded", 2)
        x1_stored = transfer("x1_stored")
        scattered = transfer("scattered", 4)
        pe = {name: event(f"pe_{name}") for name in
              ("f", "i", "h", "q", "k", "v", "aro", "wo", "x1", "mt", "hid", "lg", "rank")}
        pe_pv, pe_tr, pe_st, pe_sm = event("pe_pv", 4), event("pe_tr", 2), event("pe_st", 8), event("pe_sm", NH)
        a_f, a_i, a_q, a_k, a_ln, a_dec, a_at, a_x1, a_hid, a_re = (
            event(f"a_{n}") for n in ("f", "i", "q", "k", "ln", "dec", "at", "x1", "hid", "re"))
        a_exp, a_ov = event("a_exp", 8), event("a_ov", 4)
        v_y, v_rc, v_cum, v_new, v_v, v_q, v_k, v_mx, v_mt, v_x1, v_hid, v_lg, v_dm, v_oh, v_slot = (
            event(f"v_{n}") for n in
            ("y", "rc", "cum", "new", "v", "q", "k", "mx", "mt", "x1", "hid", "lg", "dm", "oh", "slot"))
        v_max, v_tr = event("v_max", NH), event("v_tr", 2)
        g_q, g_k, g_v, g_o, g_gate = (event(f"g_{n}") for n in ("q", "k", "v", "o", "gate"))
        v_rank = event("v_rank")
        v_steps, g_steps = sem("v_steps"), sem("g_steps")

        evacuated = {"f": (a_f, 1), "i": (a_i, 1), "q": (a_q, 1), "k": (a_k, 1), "h": (v_new, 1), "v": (v_v, 1),
                     "aro": (a_at, 1), "wo": (v_x1, 1), "x1": (a_x1, 1), "mt": (v_mt, 1), "hid": (a_hid, 1),
                     "lg": (v_lg, 1), "rank": (v_rank, 1)}
        for n in range(4):
            evacuated[f"pv{n}"] = (a_ov, n + 1)
        for n in range(2):
            evacuated[f"tr{n}"] = (v_tr, n + 1)

        def bank_free(step, job):
            at = [name for name, _ in JOBS].index(job)
            for n in range(at - 2, at - 2 * len(JOBS), -2):
                name, stage = JOBS[n % len(JOBS)]
                if name is None:
                    continue
                batch = step.batch(stage, before=1 if n < 0 else 0)
                if batch.there:
                    got = evacuated[name]
                    return [(got[0].sem, got[0].of(batch, got[1]))]
            return []

        def all_steps(eng, body, counts=()):
            for t in range(LOOP_FROM):
                body(Step(None, t))
            with eng.Fori(0, N_IN_LOOP) as i:
                for count, per in counts:
                    count.enter(i, per)
                for t in range(UNROLL):
                    body(Step(i, LOOP_FROM + t))
            for count, _ in counts:
                count.leave(N_IN_LOOP)
            for t in range(LOOP_TO, STEPS):
                body(Step(None, t))

        blk_ge = sb("blk_ge", [P, NBLK, NE])
        wsel, wrow = sb("wsel", [P, NE]), sb("wrow", [P, 2])
        pad_rows = sb("pad_rows", [P, ROW])
        cnt, nblk, endb = sb("cnt", [P, NE]), sb("nblk", [P, NE]), sb("endb", [P, NE])
        cnt_i = sb("cnt_i", [P, NE], I32)
        at_i = sb("at_i", [P, NE], I32)
        blk_e, blk_s = sb("blk_e", [P, NBLK]), sb("blk_s", [P, NBLK])
        row_tab, exp_tab = sb("row_tab", [P, NBLK], I32), sb("exp_tab", [P, NBLK], I32)
        ps_g = [t[:, 0].rearrange("p a t -> p (a t)") for t in ps_st]
        ps_u = [t[:, 1].rearrange("p a t -> p (a t)") for t in ps_st]
        ps_tx = ps_sm[0][:].rearrange("p a t -> p (a t)")
        ps_tg = ps_sm[1][:].rearrange("p a t -> p (a t)")
        ps_y = ps_job
        tables_ready, pads_in, tail_zeroed = sem("tables_ready"), sem("pads_in"), sem("tail_zeroed")
        ends_ready = sem("ends_ready")
        f_w = sem("f_w")
        pads_made = sem("pads_made")
        xb_in, added = transfer("xb_in", 1, XBUF), transfer("added", 1, XBUF)
        f_tx, f_g, f_u, f_tg, f_y = (event(f"f_{n}") for n in ("tx", "g", "u", "tg", "y"))
        f_xh, f_xT, f_silu, f_gu, f_guT, f_out = (event(f"f_{n}") for n in ("xh", "xT", "silu", "gu", "guT", "out"))

        SETUP_LOADS = [(probs[:, 0:2].rearrange("p a c t -> p (a c t)"), gate_weights), (small_sb[:], small),
                       (stage_mem[:, 0:EARLY_WEIGHTS], early_weights),
                       (rope_tok[:].rearrange("p a b t -> p (a b t)"), rope_tokens),
                       (late_w[:].rearrange("p n k d -> p (n k d)"), late_weights)]
        GATE_CONSTS, CONSTS = 16 * 2, 16 * len(SETUP_LOADS[2:])
        w1_sb, w2_sb = probs[:, 0, :, :], probs[:, 1, :, :]
        SETUP_DONE = 7

        def ffn_steps(eng, body, *stages):
            def turn(i, base):
                for k in range(XBUF):
                    body(*(Batch(i, base + k - s, NBLK, XBUF) for s in stages))
            turn(None, 0)
            with eng.Fori(0, NBLK // XBUF - 1) as i:
                turn(i, XBUF)
            if max(stages):
                turn(None, NBLK)

        sp_waits_passed, pool_waits_passed = sem("sp_waits_passed"), sem("pool_waits_passed")

        def part_of(w, n):
            words = w.shape[1] // PARTS
            return w[:, n * words:n * words + words]

        block = ctx.enter_context(nc.Block())

        @block.sync
        def _(sp):
            for dst, src in SETUP_LOADS[:2]:
                sp.dma_start(dst, src).then_inc(gate_in, 16)
            for dst, src in SETUP_LOADS[2:]:
                sp.dma_start(dst, src).then_inc(consts_in, 16)

            def load_experts(to, frm, n, done):
                sp.dma_start(part_of(to, n), part_of(frm, n)).then_inc(done, 16)

            def step(s):
                a, b, m, c, d = (s.batch(n) for n in ("y", "qk", "max", "out", "rec"))
                if c.there:
                    if c.has(1):
                        sp.wait_ge(v_x1.sem, v_x1.of(c.back(1)))
                    sp.sem_inc(sp_waits_passed, 1)
                    sp.dma_start(
                        x_res[:], xT[:, bass.ds(c.index, 1), :].rearrange("(c p) o t -> p (o c) t", p=P)).then_inc(res_loaded.sems[c.par], 16)
                if b.there:
                    if b.has(1):
                        sp.wait_ge(rows_loaded.sems[b.back(1).par], rows_loaded.of(b.back(1)))
                    sp.sem_inc(sp_waits_passed, 1)
                    sp.wait_ge(v_q.sem, v_q.of(b))
                    sp.dma_start(q_parts.rearrange("x p t -> p x t"),
                                 q_split[:].rearrange("p c (a t) -> p (c a) t", a=2)).then_inc(q_stored.sems[b.par], 16)
                    if b.has(2):
                        sp.wait_ge(pe_st.sem, pe_st.of(b.back(2)))
                    sp.sem_inc(sp_waits_passed, 1)
                    sp.wait_ge(q_stored.sems[b.par], q_stored.of(b))
                    qv = q_parts.rearrange("x (i h) t -> (x i) (h t)", h=NH)
                    row = 0
                    for parts in (3, 2, 1):
                        n = parts * HD
                        sp.dma_start(
                            q_rows[row:row + n, b.par].rearrange("p h t -> p (h t)"), qv[0:n, :]).then_inc(rows_loaded.sems[b.par], 16)
                        row += n
                if a.there:
                    if a.has(1):
                        sp.wait_ge(v_y.sem, v_y.of(a.back(1)))
                    sp.sem_inc(sp_waits_passed, 1)
                    sp.dma_start(
                        x_in[:], xT[:, bass.ds(a.index, 1), :].rearrange("(c p) o t -> p (o c) t", p=P)).then_inc(x_loaded.sems[a.par], 16)
                if b.there:
                    sp.wait_ge(v_k.sem, v_k.of(b))
                    sp.sem_inc(sp_waits_passed, 1)
                    sp.dma_start(k_parts.rearrange("x p t -> p x t"),
                                 k_split[:].rearrange("p c (a t) -> p (c a) t", a=2)).then_inc(k_stored.sems[b.par], 16)
                    sp.wait_ge(k_stored.sems[b.par], k_stored.of(b))
                    kv = k_parts.rearrange("x (i h) t -> (x i) (h t)", h=NH)
                    for n, part in enumerate((0, 0, 0, 1, 1, 2)):
                        sp.dma_start(
                            k_rows[n * HD:n * HD + HD, b.par].rearrange("p h t -> p (h t)"),
                            kv[part * HD:part * HD + HD, :]).then_inc(rows_loaded.sems[b.par], 16)
                if m.there:
                    if m.has(2):
                        sp.wait_ge(pe_st.sem, pe_st.of(m.back(2)))
                    sp.sem_inc(sp_waits_passed, 1)
                    sp.wait_ge(v_mt.sem, v_mt.of(m))
                    for part in range(2):
                        sp.dma_start(
                            q_rows[SPLIT_ROWS + part:SPLIT_ROWS + part + 1, m.par, :, :],
                            mx_rows[NH * part:NH * part + NH, :]).then_inc(max_loaded.sems[m.par], 16)
                if d.there:
                    sp.wait_ge(a_x1.sem, a_x1.of(d))
                    sp.sem_inc(sp_waits_passed, 1)
                    sp.dma_start(
                        out[bass.ds(d.index * NT, NT), :].rearrange("(c p) f -> p c f", p=P), x1_row[:]).then_inc(x1_stored.sems[d.par], 16)

            def step_and_weights(s):
                step(s)
                if s.i is None and s.offset == 0:
                    sp.wait_ge(pads_made, 1)
                    sp.dma_start(sorted_rows[PAD_ROW:PAD_ROW + P, :], pad_rows[:]).then_inc(tail_zeroed, 16)
                    sp.dma_start(out[TOKENS:TOKENS + P, :], pad_rows[:, 0:D]).then_inc(tail_zeroed, 16)
                if s.i is None and 4 <= s.offset < 4 + PARTS:
                    load_experts(gate_mem, w_gate, s.offset - 4, gate_w_in)
                if s.i is None and s.offset == NB + STAGES["max"]:
                    sp.wait_ge(pe["v"].sem, pe["v"].of(Batch(None, NB - 1)))
                    for n in range(PARTS):
                        load_experts(stage_mem, w_up, n, up_w_in)
                if s.i is None and s.offset == NB + STAGES["att"]:
                    sp.wait_ge(pe_st.sem, pe_st.of(Batch(None, NB - 1)))
                    for n in range(PARTS):
                        load_experts(wd_all, w_down, n, down_w_in)

            all_steps(sp, step_and_weights)

            sp.wait_ge(ends_ready, 1)
            for e in range(NE):
                row = sp.value_load(at_i[0:1, e:e + 1], min_val=0, max_val=SORTED - P)
                sp.dma_start(sorted_rows[bass.ds(row, P), :], pad_rows[:]).then_inc(pads_in, 16)
            sp.wait_ge(pads_in, 16 * NE)
            sp.wait_ge(tail_zeroed, 32)
            sp.wait_ge(tables_ready, 1)
            for n in range(2):
                sp.wait_ge(scattered.sems[Batch(None, NB - 1 - n).par], scattered.of(Batch(None, NB - 1 - n)))
                sp.wait_ge(x1_stored.sems[Batch(None, NB - 1 - n).par], x1_stored.of(Batch(None, NB - 1 - n)))

            def load_block(n):
                if n.has(XBUF):
                    sp.wait_ge(added.sems[n.back(XBUF).par], added.of(n.back(XBUF)))
                sp.sem_inc(sp_waits_passed, 1)
                row = sp.value_load(row_tab[0:1, bass.ds(n.index, 1)], min_val=0, max_val=PAD_ROW)
                sp.dma_start(xb[:, n.par], sorted_rows[bass.ds(row, P), :]).then_inc(xb_in.sems[n.par], 16)

            for k in range(XBUF):
                load_block(Batch(None, k, NBLK, XBUF))
            with sp.Fori(0, NBLK // XBUF - 1) as i:
                for k in range(XBUF):
                    load_block(Batch(i, XBUF + k, NBLK, XBUF))
            for k in range(XBUF):
                sp.wait_ge(added.sems[k], 16 * NBLK // XBUF)

        @block.gpsimd
        def _(pool):
            steps = Count()

            def products(x, tables):
                pool.tensor_tensor(t1[:], x, tables[:, 0], ALU.mult).then_inc(g_steps, 1)
                pool.tensor_tensor(t2[:], x, tables[:, 1], ALU.mult).then_inc(g_steps, 1)
                pool.wait_ge(g_steps, steps.up(2))

            def rope_by_feature(x, to, event, batch):
                products(x, rqk)
                pool.tensor_tensor(to[:, 0:NT], t1[:, 0:NT], t1[:, NT:], ALU.subtract).then_inc(g_steps, 1)
                pool.tensor_tensor(to[:, NT:], t2[:, 0:NT], t2[:, NT:], ALU.add).then_inc(event.sem, 1)
                pool.wait_ge(g_steps, steps.up(1))
                pool.wait_ge(event.sem, event.of(batch))

            def step(s):
                b, m, c, d, e = (s.batch(n) for n in ("qk", "max", "out", "rec", "route"))
                if b.there:
                    pool.wait_ge(a_q.sem, a_q.of(b))
                    if b.has(1):
                        pool.wait_ge(v_q.sem, v_q.of(b.back(1)))
                    rope_by_feature(q_lin[:], q_rope, g_q, b)
                if d.there:
                    pool.wait_ge(v_rc.sem, v_rc.of(d))
                    pool.tensor_tensor(fg[:], fg[:], rc[:], ALU.mult)
                    pool.tensor_tensor(ig[:], ig[:], rc[:], ALU.mult).then_inc(g_gate.sem, 1)
                if c.there:
                    pool.wait_ge(v_tr.sem, v_tr.of(c))
                    products(o_norm[:].rearrange("p c f -> p (c f)"), ro)
                    if c.has(1):
                        pool.wait_ge(pe["aro"].sem, pe["aro"].of(c.back(1)))
                    to = o_rope[:].rearrange("p c (h a i) -> p (c h) a i", h=NH, a=2)
                    t1v, t2v = (t[:].rearrange("p (g i a) -> p g i a", i=HALF, a=2) for t in (t1, t2))
                    pool.tensor_tensor(to[:, :, 0], t1v[:, :, :, 0], t1v[:, :, :, 1], ALU.add).then_inc(g_steps, 1)
                    pool.tensor_tensor(to[:, :, 1], t2v[:, :, :, 0], t2v[:, :, :, 1], ALU.add).then_inc(g_o.sem, 1)
                    pool.wait_ge(g_steps, steps.up(1))
                    pool.wait_ge(g_o.sem, g_o.of(c))
                if b.there:
                    pool.wait_ge(a_k.sem, a_k.of(b))
                    if b.has(1):
                        pool.wait_ge(v_k.sem, v_k.of(b.back(1)))
                    rope_by_feature(k_lin[:], k_rope, g_k, b)
                if m.there:
                    pool.wait_ge(v_v.sem, v_v.of(m))
                    products(v_lin[:], rv)
                    if m.has(2):
                        pool.wait_ge(pe_pv.sem, pe_pv.of(m.back(2)))
                    va = v_aug[:, m.par].rearrange("p (c h) k -> p c h k", c=2)
                    t1v, t2v = (t[:].rearrange("p (c a h i) -> p c a h i", c=2, a=2, i=HALF) for t in (t1, t2))
                    pool.tensor_tensor(va[:, :, :, 0:HALF], t1v[:, :, 0], t1v[:, :, 1],
                                                    ALU.subtract).then_inc(g_steps, 1)
                    pool.tensor_tensor(va[:, :, :, HALF:HD], t2v[:, :, 0], t2v[:, :, 1],
                                                  ALU.add).then_inc(g_v.sem, 1)
                    pool.wait_ge(g_steps, steps.up(1))
                    pool.wait_ge(g_v.sem, g_v.of(m))
                if s.i is None and s.offset == NB - 1 + STAGES["rec"]:
                    for n in range(PARTS):
                        pool.wait_ge(low_begun, n + 1)
                        pool.tensor_tensor(part_of(wg_low, n), part_of(gate_mem, n), part_of(wg_low, n).bitcast(F32),
                                           ALU.subtract).then_inc(low_by_pool, 1)
                if e.there:
                    pool.wait_ge(v_slot.sem, v_slot.of(e))
                    pool.wait_ge(a_hid.sem, a_hid.of(e))
                    pool.sem_inc(pool_waits_passed, 1)
                    for choice in range(2):
                        for tc in range(2):
                            pool.indirect_dma_start(
                                out=sorted_rows, out_offset=bass.IndirectOffsetOnAxis(
                                    ap=slots[:, e.par, choice, tc:tc + 1], axis=0),
                                in_=hrow[:, e.par, tc], in_offset=None).then_inc(scattered.sems[e.par], 16)

            pool.wait_ge(gate_in, GATE_CONSTS)
            pool.wait_ge(consts_in, CONSTS)
            pool.wait_ge(setup_done, SETUP_DONE)
            all_steps(pool, step, [(steps, 4 * UNROLL * 3)])

            pool.wait_ge(low_begun, 2 * PARTS)
            pool.tensor_tensor(part_of(wu_low, PARTS - 1), part_of(stage_mem, PARTS - 1),
                               part_of(wu_low, PARTS - 1).bitcast(F32), ALU.subtract).then_inc(low_by_pool, 1)
            pool.wait_ge(tail_zeroed, 32)
            for n in range(2):
                pool.wait_ge(x1_stored.sems[Batch(None, NB - 1 - n).par], x1_stored.of(Batch(None, NB - 1 - n)))

            def add_block(n):
                pool.wait_ge(f_out.sem, f_out.of(n))
                if n.has(1):
                    pool.wait_ge(added.sems[n.back(1).par], added.of(n.back(1)))
                pool.sem_inc(pool_waits_passed, 1)
                pool.indirect_dma_start(
                    out=out, out_offset=bass.IndirectOffsetOnAxis(
                        ap=xb[:, n.par, ROW_ID:ROW_ID + 1].bitcast(U32), axis=0),
                    in_=ysb[:, n.par % 2], in_offset=None, compute_op=ALU.add).then_inc(added.sems[n.par], 16)

            for k in range(XBUF):
                add_block(Batch(None, k, NBLK, XBUF))
            with pool.Fori(0, NBLK // XBUF - 1) as i:
                for k in range(XBUF):
                    add_block(Batch(i, XBUF + k, NBLK, XBUF))

        @block.scalar
        def _(act):
            act.wait_ge(gate_pe, 1)
            for c in range(2):
                act.activation(gh[:, c], ps_job[0][:, c * NB:c * NB + NB], ACT.Identity, bias=bias[:, 6, c:c + 1])
            for c in range(2):
                act.activation(gs[:, c], ps_job[0][:, c * NB:c * NB + NB], ACT.Sigmoid,
                               bias=bias[:, 6, c:c + 1]).then_inc(gate_act, 1)
            act.wait_ge(gate_pe, 2)
            for c in range(2):
                act.activation(g1[:, c], ps_job[1][:, c * NB:c * NB + NB], ACT.Sigmoid,
                               bias=bias[:, 7, c:c + 1]).then_inc(gate_act, 1)

            def by_feature(to, frm, func, b):
                for c in range(2):
                    last = act.activation(to[:, c * NT:c * NT + NT], frm[:, c * NT:c * NT + NT], func, bias=bias[:, b, c:c + 1])
                return last

            def exp(s, u):
                if s.there:
                    act.wait_ge(pe_st.sem, pe_st.of(s, u + 1))
                    if u >= 4:
                        act.wait_ge(pe_pv.sem, pe_pv.of(s, (u - 4) // 2 + 1))
                    else:
                        if s.has(1):
                            act.wait_ge(pe_pv.sem, pe_pv.of(s.back(1), 3 + u // 2))
                    at = 2 * u % 8
                    act.activation(probs[:, at:at + 2], ps_st[u % 2][:], ACT.Exp, scale=SCALE).then_inc(a_exp.sem, 1)

            def outputs(b, g):
                if b.there:
                    act.wait_ge(pe_pv.sem, pe_pv.of(b, g + 1))
                    if b.has(1):
                        act.wait_ge(pe_tr.sem, pe_tr.of(b.back(1)))
                    act.copy(o_raw[:, g], bank[f"pv{g}"][:, 0:NT]).then_inc(a_ov.sem, 1)

            def step(s):
                b, a, c, d, e = (s.batch(n) for n in ("qk", "att", "out", "rec", "route"))
                if d.there:
                    act.wait_ge(pe["f"].sem, pe["f"].of(d))
                    if d.has(1):
                        act.wait_ge(a_ln.sem, a_ln.of(d.back(1)))
                    by_feature(fg[:].rearrange("p c t -> p (c t)"), bank["f"], ACT.Sigmoid, 3).then_inc(a_f.sem, 1)
                if d.there:
                    act.wait_ge(pe["i"].sem, pe["i"].of(d))
                    if d.has(1):
                        act.wait_ge(v_new.sem, v_new.of(d.back(1)))
                    by_feature(ig[:].rearrange("p c t -> p (c t)"), bank["i"], ACT.Sigmoid, 4).then_inc(a_i.sem, 1)
                if b.there:
                    act.wait_ge(pe["q"].sem, pe["q"].of(b))
                    if b.has(1):
                        act.wait_ge(g_q.sem, g_q.of(b.back(1)))
                    by_feature(q_lin, bank["q"], ACT.Identity, 0).then_inc(a_q.sem, 1)
                outputs(c, 3)
                exp(a, 0)
                exp(a, 1)
                if b.there:
                    act.wait_ge(pe["k"].sem, pe["k"].of(b))
                    if b.has(1):
                        act.wait_ge(g_k.sem, g_k.of(b.back(1)))
                    by_feature(k_lin, bank["k"], ACT.Identity, 1).then_inc(a_k.sem, 1)
                exp(a, 2)
                outputs(a, 0)
                exp(a, 3)
                if d.there:
                    act.wait_ge(g_gate.sem, g_gate.of(d))
                    if d.has(1):
                        act.wait_ge(v_cum.sem, v_cum.of(d.back(1)))
                    act.activation(lr[:], fg[:], ACT.Ln, bias=eps_sb[:, 0:1]).then_inc(a_ln.sem, 1)
                exp(a, 4)
                exp(a, 5)
                if c.there:
                    act.wait_ge(pe["aro"].sem, pe["aro"].of(c))
                    if c.has(1):
                        act.wait_ge(pe["wo"].sem, pe["wo"].of(c.back(1)))
                    act.copy(o_T[:].rearrange("p c t -> p (c t)"), bank["aro"][:, 0:2 * NT]).then_inc(a_at.sem, 1)
                exp(a, 6)
                if d.there:
                    act.wait_ge(v_cum.sem, v_cum.of(d))
                    if d.has(1):
                        act.wait_ge(v_hid.sem, v_hid.of(d.back(1)))
                    for k in range(2):
                        act.activation(scaling[:, k], lc[:, k, 0:NT], ACT.Exp, scale=-1.0, bias=lc[:, k, NT:NT + 1])
                    act.activation(decay[:], lc[:, :, 1:NT + 1], ACT.Exp).then_inc(a_dec.sem, 1)
                outputs(a, 1)
                if e.there:
                    act.wait_ge(v_dm.sem, v_dm.of(e))
                    act.activation(ex[:], ex[:], ACT.Exp).then_inc(a_re.sem, 1)
                outputs(a, 2)
                exp(a, 7)
                if d.there:
                    act.wait_ge(pe["x1"].sem, pe["x1"].of(d))
                    if d.has(1):
                        act.wait_ge(x1_stored.sems[d.back(1).par], x1_stored.of(d.back(1)))
                    act.copy(x1_row[:].rearrange("p c t -> p (c t)"), bank["x1"][:, 0:2 * NT]).then_inc(a_x1.sem, 1)
                if d.there:
                    act.wait_ge(pe["hid"].sem, pe["hid"].of(d))
                    if d.has(2):
                        act.wait_ge(scattered.sems[d.back(2).par], scattered.of(d.back(2)))
                    act.copy(hrow[:, d.par, :, 0:D], bank["hid"][:, 0:2 * NT].rearrange("p (c f) -> p c f", c=2)
                    ).then_inc(a_hid.sem, 1)

            act.wait_ge(setup_done, SETUP_DONE)
            def step_and_weights(s):
                step(s)
                if s.i is None and s.offset == NB - 1 + STAGES["out"]:
                    act.wait_ge(pe["wo"].sem, pe["wo"].of(Batch(None, NB - 1)))
                    act.wait_ge(gate_w_in, 16 * PARTS)
                    for n in range(PARTS):
                        act.copy(part_of(wg_low, n), part_of(gate_mem, n)).then_inc(low_begun, 1)

            all_steps(act, step_and_weights)

            act.wait_ge(pe["lg"].sem, pe["lg"].of(Batch(None, NB - 1)))
            act.wait_ge(v_lg.sem, v_lg.of(Batch(None, NB - 1)))
            act.wait_ge(x1_stored.sems[Batch(None, NB - 1).par], x1_stored.of(Batch(None, NB - 1)))
            act.wait_ge(up_w_in, 16 * PARTS)
            for n in range(PARTS):
                act.copy(part_of(wu_low, n), part_of(stage_mem, n)).then_inc(low_begun, 1)
            for n in range(PARTS):
                act.wait_ge(low_by_pool, n + 1)
                act.copy(part_of(wg_high, n), part_of(gate_mem, n)).then_inc(high_made, 1)
            for n in range(PARTS - 1):
                act.wait_ge(low_by_vector, n + 1)
                act.copy(part_of(wu_high, n), part_of(stage_mem, n)).then_inc(high_made, 1)
            act.wait_ge(low_by_pool, PARTS + 1)
            act.copy(part_of(wu_high, PARTS - 1), part_of(stage_mem, PARTS - 1)).then_inc(high_made, 1)

            def ffn(n_g, n_t):
                if n_t.there:
                    act.wait_ge(f_tg.sem, f_tg.of(n_t))
                    if n_t.has(1):
                        act.wait_ge(f_y.sem, f_y.of(n_t.back(1)))
                    act.copy(gu_T[:].rearrange("p a t -> p (a t)"), ps_tg).then_inc(f_guT.sem, 1)
                if n_g.there:
                    act.wait_ge(f_g.sem, f_g.of(n_g))
                    if n_g.has(2):
                        act.wait_ge(f_gu.sem, f_gu.of(n_g.back(2)))
                    act.activation(silu[:, n_g.par % 2], ps_g[n_g.par % 2], ACT.Silu).then_inc(f_silu.sem, 1)

            ffn_steps(act, ffn, 0, 1)

        @block.vector
        def _(v):
            steps = Count()

            def tt(o, a, b, op):
                return v.tensor_tensor(o, a, b, op)

            v.memset(pad_rows[:], 0.0).then_inc(gate_v, 1)
            v.memset(ones_row[:], 1.0).then_inc(setup_done, 1)
            v.memset(eps_sb[:], EPS).then_inc(setup_done, 1)
            v.memset(v_aug.rearrange("p a g k -> p (a g) k")[:, :, HD:], 1.0).then_inc(setup_done, 1)
            v.memset(k_rows[SPLIT_ROWS:SCORE_ROWS], -1.0).then_inc(setup_done, 1)
            v.memset(lc[:, :, 0:1], 0.0).then_inc(setup_done, 1)
            v.memset(hrow[:], 0.0).then_inc(setup_done, 1)
            v.wait_ge(gate_in, GATE_CONSTS)
            v.tensor_copy(ident_b[:], ident).then_inc(gate_v, 1)
            v.tensor_copy(counters[:, 0:P], upper).then_inc(gate_v, 1)
            v.tensor_copy(counters[:, P:2 * P], ones).then_inc(gate_v, 1)
            v.tensor_copy(tid[:], token_p).then_inc(gate_v, 1)
            v.tensor_copy(at_e[:], region_e).then_inc(gate_v, 1)
            v.wait_ge(gate_v, 6)
            v.tensor_scalar(pad_rows[:, ROW_ID:ROW_ID + 1].bitcast(U32), tid[:, 0:1], float(TOKENS), None,
                            ALU.add).then_inc(pads_made, 1)
            v.wait_ge(gate_act, 2)
            tt(gh[:], gh[:], gs[:], ALU.mult).then_inc(gate_v, 1)
            v.wait_ge(gate_act, 4)
            v.tensor_scalar(g1[:], g1[:], 1.0, None, ALU.add).then_inc(setup_done, 1)
            v.wait_ge(setup_done, SETUP_DONE)
            v.wait_ge(pads_made, 1)

            def row_max(m, h):
                if m.there:
                    if h == 0 and m.has(1):
                        v.wait_ge(v_mx.sem, v_mx.of(m.back(1)))
                    v.wait_ge(pe_sm.sem, pe_sm.of(m, h + 1))
                    v.tensor_reduce(mx[:, :, h], ps_sm[h % 2][:], AX.X, ALU.max).then_inc(v_max.sem, 1)

            def split(b, x, to, ready, stored, done):
                v.wait_ge(ready.sem, ready.of(b))
                if b.has(1):
                    v.wait_ge(stored.sems[b.back(1).par], stored.of(b.back(1)))
                v.tensor_copy(to[:, 0], x[:]).then_inc(v_steps, 1)
                v.wait_ge(v_steps, steps.up(1))
                tt(rest[:], x[:], to[:, 0], ALU.subtract).then_inc(v_steps, 1)
                v.wait_ge(v_steps, steps.up(1))
                v.tensor_copy(to[:, 1], rest[:]).then_inc(v_steps, 1)
                v.wait_ge(v_steps, steps.up(1))
                tt(to[:, 2], rest[:], to[:, 1], ALU.subtract).then_inc(done.sem, 1)
                v.wait_ge(done.sem, done.of(b))

            def wide(x):
                return x[:].unsqueeze(2).to_broadcast([P, 2, NE])

            def narrow(x):
                return x.unsqueeze(1).to_broadcast([P, 2, NE])

            def choose(onehot, top):
                tt(r_a[:], lg[:], wide(top), ALU.is_equal).then_inc(v_steps, 1)
                v.wait_ge(v_steps, steps.up(1))
                v.scalar_tensor_tensor(out=r_b[:], in0=r_a[:], scalar=-2.0 * NE, in1=narrow(iota_e),
                                                       op0=ALU.mult, op1=ALU.add).then_inc(v_steps, 1)
                v.wait_ge(v_steps, steps.up(1))
                v.tensor_reduce(mv[:], r_b[:], AX.X, ALU.min).then_inc(v_steps, 1)
                v.wait_ge(v_steps, steps.up(1))
                tt(onehot[:], r_b[:], wide(mv), ALU.is_equal).then_inc(v_steps, 1)
                v.wait_ge(v_steps, steps.up(1))

            def step(s):
                y_, b, m, c, d, e = (s.batch(n) for n in ("y", "qk", "max", "out", "rec", "route"))
                row_max(m, 0)
                row_max(m, 1)
                if d.there:
                    v.wait_ge(a_f.sem, a_f.of(d))
                    v.wait_ge(a_i.sem, a_i.of(d))
                    if d.has(1):
                        v.wait_ge(g_gate.sem, g_gate.of(d.back(1)))
                    v.scalar_tensor_tensor(out=rc[:], in0=fg[:], scalar=EPS, in1=ig[:],
                                                           op0=ALU.add, op1=ALU.add).then_inc(v_steps, 1)
                    v.wait_ge(v_steps, steps.up(1))
                    v.reciprocal(rc[:, 0], rc[:, 0])
                row_max(m, 2)
                if d.there:
                    v.reciprocal(rc[:, 1], rc[:, 1]).then_inc(v_rc.sem, 1)
                row_max(m, 3)
                if c.there:
                    if c.has(1):
                        v.wait_ge(g_o.sem, g_o.of(c.back(1)))
                    for n in range(2):
                        v.wait_ge(pe_tr.sem, pe_tr.of(c, n + 1))
                        got = bank[f"tr{n}"][:].rearrange("p (h k) -> p h k", h=NH)
                        v.reciprocal(o_den[:, n], got[:, :, HD]).then_inc(v_steps, 1)
                        v.wait_ge(v_steps, steps.up(1))
                        tt(o_norm[:, n].rearrange("p (h k) -> p h k", h=NH), got[:, :, 0:HD],
                                       o_den[:, n].unsqueeze(2).to_broadcast([P, NH, HD]), ALU.mult).then_inc(v_tr.sem, 1)
                row_max(m, 4)
                row_max(m, 5)
                if b.there:
                    split(b, q_rope, q_split, g_q, q_stored, v_q)
                row_max(m, 6)
                if e.there:
                    v.wait_ge(v_lg.sem, v_lg.of(e))
                    if e.has(1):
                        v.wait_ge(v_slot.sem, v_slot.of(e.back(1)))
                    v.tensor_reduce(m1[:], lg[:], AX.X, ALU.max).then_inc(v_steps, 1)
                    v.wait_ge(v_steps, steps.up(1))
                    choose(oh1, m1)
                    v.scalar_tensor_tensor(out=lg[:], in0=oh1[:], scalar=-1e30, in1=lg[:],
                                                           op0=ALU.mult, op1=ALU.add).then_inc(v_steps, 1)
                    v.wait_ge(v_steps, steps.up(1))
                    v.tensor_reduce(m2[:], lg[:], AX.X, ALU.max).then_inc(v_steps, 1)
                    v.wait_ge(v_steps, steps.up(1))
                    choose(oh2, m2)
                    tt(oh_b[:], oh1[:], oh2[:], ALU.add).then_inc(v_oh.sem, 1)
                    tt(ex[:], m2[:], m1[:], ALU.subtract).then_inc(v_dm.sem, 1)
                row_max(m, 7)
                if m.there:
                    v.wait_ge(pe["v"].sem, pe["v"].of(m))
                    if m.has(1):
                        v.wait_ge(g_v.sem, g_v.of(m.back(1)))
                    tt(v_lin[:].rearrange("p (c f) -> p c f", c=2),
                                  bank["v"][:].rearrange("p (c f) -> p c f", c=2),
                                  bv_sb.unsqueeze(1).to_broadcast([P, 2, D]), ALU.add).then_inc(v_v.sem, 1)
                if d.there:
                    v.wait_ge(pe["h"].sem, pe["h"].of(d))
                    v.wait_ge(g_gate.sem, g_gate.of(d))
                    if d.has(1):
                        v.wait_ge(v_hid.sem, v_hid.of(d.back(1)))
                    for k in range(2):
                        last = v.scalar_tensor_tensor(out=info[:, k], in0=bank["h"][:, k * NT:k * NT + NT],
                                                      scalar=bias[:, 5, k:k + 1], in1=ig[:, k],
                                                      op0=ALU.add, op1=ALU.mult)
                    last.then_inc(v_new.sem, 1)
                row_max(m, 8)
                if d.there:
                    v.wait_ge(a_ln.sem, a_ln.of(d))
                    if d.has(1):
                        v.wait_ge(a_dec.sem, a_dec.of(d.back(1)))
                    for k in range(2):
                        last = v.tensor_tensor_scan(lc[:, k, 1:NT + 1], ones_row[:], lr[:, k], 0.0, ALU.mult, ALU.add)
                    last.then_inc(v_cum.sem, 1)
                row_max(m, 9)
                if b.there:
                    split(b, k_rope, k_split, g_k, k_stored, v_k)
                row_max(m, 10)
                if d.there:
                    v.wait_ge(a_dec.sem, a_dec.of(d))
                    v.wait_ge(v_new.sem, v_new.of(d))
                    tt(info[:], info[:], scaling[:], ALU.mult).then_inc(v_steps, 1)
                    v.wait_ge(v_steps, steps.up(1))
                    if d.has(1):
                        v.wait_ge(pe["lg"].sem, pe["lg"].of(d.back(1)))
                    for k in range(2):
                        v.tensor_tensor_scan(hid[:, k], ones_row[:], info[:, k], 0.0, ALU.mult, ALU.add
                        ).then_inc(v_steps, 1)
                    v.wait_ge(v_steps, steps.up(2))
                    for k in range(2):
                        last = v.scalar_tensor_tensor(out=hid[:, k], in0=decay[:, k],
                                                      scalar=cond_sb[:, k, bass.ds(d.index, 1)], in1=hid[:, k],
                                                      op0=ALU.mult, op1=ALU.add)
                    last.then_inc(v_hid.sem, 1)
                if e.there:
                    v.wait_ge(pe["rank"].sem, pe["rank"].of(e))
                    tt(r_c[:], bank["rank"][:, 0:2 * NE].rearrange("p (c k) -> p c k", c=2),
                       narrow(at_e[:]), ALU.add).then_inc(v_steps, 1)
                    v.wait_ge(v_steps, steps.up(1))
                    tt(at_e[:], at_e[:], bank["rank"][:, 2 * NE:3 * NE], ALU.add).then_inc(v_rank.sem, 1)
                row_max(m, 11)
                row_max(m, 12)
                row_max(m, 13)
                if c.there:
                    v.wait_ge(pe["wo"].sem, pe["wo"].of(c))
                    v.wait_ge(res_loaded.sems[c.par], res_loaded.of(c))
                    if c.has(2):
                        v.wait_ge(pe["x1"].sem, pe["x1"].of(c.back(2)))
                    for k in range(2):
                        last = v.scalar_tensor_tensor(out=x1[:, c.par, k], in0=bank["wo"][:, k * NT:k * NT + NT],
                                                      scalar=bias[:, 2, k:k + 1], in1=x_res[:, k],
                                                      op0=ALU.add, op1=ALU.add)
                    last.then_inc(v_x1.sem, 1)
                row_max(m, 14)
                row_max(m, 15)
                if m.there:
                    v.wait_ge(v_max.sem, v_max.of(m))
                    if m.has(1):
                        v.wait_ge(pe["mt"].sem, pe["mt"].of(m.back(1)))
                    v.tensor_copy(mx_split[:, :, 0], mx[:]).then_inc(v_steps, 1)
                    v.wait_ge(v_steps, steps.up(1))
                    tt(mx_split[:, :, 1], mx[:], mx_split[:, :, 0], ALU.subtract).then_inc(v_mx.sem, 1)
                if d.there:
                    v.wait_ge(pe["lg"].sem, pe["lg"].of(d))
                    if d.has(1):
                        v.wait_ge(v_oh.sem, v_oh.of(d.back(1)))
                    v.tensor_copy(lg[:].rearrange("p c k -> p (c k)"), bank["lg"][:, 0:2 * NE]).then_inc(v_lg.sem, 1)
                if y_.there:
                    v.wait_ge(x_loaded.sems[y_.par], x_loaded.of(y_))
                    if y_.has(2):
                        v.wait_ge(pe["v"].sem, pe["v"].of(y_.back(2)))
                    for k in range(2):
                        last = v.tensor_scalar(y[:, y_.par, k], x_in[:, k], g1[:, k, bass.ds(y_.index, 1)],
                                               None, ALU.mult)
                    last.then_inc(v_y.sem, 1)
                if m.there:
                    v.wait_ge(pe["mt"].sem, pe["mt"].of(m))
                    if m.has(1):
                        v.wait_ge(max_loaded.sems[m.back(1).par], max_loaded.of(m.back(1)))
                    v.tensor_copy(mx_rows[:], bank["mt"][0:2 * NH, 0:NT // 2].bitcast(BF16)).then_inc(v_mt.sem, 1)
                if e.there:
                    if e.has(2):
                        v.wait_ge(scattered.sems[e.back(2).par], scattered.of(e.back(2)))
                    v.wait_ge(a_re.sem, a_re.of(e))
                    tt(r_a[:], r_c[:], oh1[:], ALU.mult).then_inc(v_steps, 1)
                    steps.up(1)
                    tt(r_b[:], r_c[:], oh2[:], ALU.mult).then_inc(v_steps, 1)
                    v.wait_ge(v_steps, steps.up(1))
                    v.tensor_reduce(sl[:, 0], r_a[:], AX.X, ALU.add).then_inc(v_steps, 1)
                    steps.up(1)
                    v.tensor_reduce(sl[:, 1], r_b[:], AX.X, ALU.add).then_inc(v_steps, 1)
                    v.wait_ge(v_steps, steps.up(1))
                    v.tensor_copy(slots[:, e.par], sl[:]).then_inc(v_steps, 1)
                    steps.up(1)
                    v.tensor_scalar(w1c[:], ex[:], 1.0, None, ALU.add).then_inc(v_steps, 1)
                    v.wait_ge(v_steps, steps.up(1))
                    v.reciprocal(w1c[:], w1c[:]).then_inc(v_steps, 1)
                    v.wait_ge(v_steps, steps.up(1))
                    tt(w2c[:], ex[:], w1c[:], ALU.mult).then_inc(v_steps, 1)
                    v.wait_ge(v_steps, steps.up(1))
                    tt(oh1[:], oh1[:], wide(w1c), ALU.mult).then_inc(v_steps, 1)
                    steps.up(1)
                    tt(oh2[:], oh2[:], wide(w2c), ALU.mult).then_inc(v_steps, 1)
                    v.wait_ge(v_steps, steps.up(1))
                    tt(hrow[:, e.par, :, ROW_W:ROW_W + NE], oh1[:], oh2[:], ALU.add).then_inc(v_steps, 1)
                    steps.up(1)
                    v.tensor_copy(hrow[:, e.par, :, ROW_ID:ROW_ID + 1].bitcast(U32),
                                                  tid[:].unsqueeze(2)).then_inc(v_steps, 1)
                    v.wait_ge(v_steps, steps.up(1))
                    v.tensor_scalar(tid[:], tid[:], float(NT), None, ALU.add).then_inc(v_slot.sem, 1)

            all_steps(v, step, [(steps, V_STEPS * UNROLL)])

            v.wait_ge(v_rank.sem, v_rank.of(Batch(None, NB - 1)))
            v.tensor_copy(at_i[:], at_e[:]).then_inc(ends_ready, 1)
            tt(cnt[:], at_e[:], region_e, ALU.subtract).then_inc(v_steps, 1)
            v.wait_ge(v_steps, steps.up(1))
            v.tensor_scalar(cnt[:], cnt[:], float(P - 1), None, ALU.add).then_inc(v_steps, 1)
            v.wait_ge(v_steps, steps.up(1))
            v.tensor_copy(cnt_i[:], cnt[:]).then_inc(v_steps, 1)
            v.wait_ge(v_steps, steps.up(1))
            v.tensor_scalar(cnt_i[:], cnt_i[:], P.bit_length() - 1, None, ALU.logical_shift_right
            ).then_inc(v_steps, 1)
            v.wait_ge(v_steps, steps.up(1))
            v.tensor_copy(nblk[:], cnt_i[:]).then_inc(v_steps, 1)
            v.wait_ge(v_steps, steps.up(1))
            v.tensor_tensor_scan(endb[:], ones_row[:, 0:NE], nblk[:], 0.0, ALU.mult, ALU.add).then_inc(v_steps, 1)
            v.wait_ge(v_steps, steps.up(1))

            def by_block(x):
                return x.unsqueeze(1).to_broadcast([P, NBLK, NE])

            def by_expert(x):
                return x.unsqueeze(2).to_broadcast([P, NBLK, NE])

            tt(blk_ge[:], by_expert(blk), by_block(endb[:]), ALU.is_ge).then_inc(v_steps, 1)
            v.wait_ge(v_steps, steps.up(1))
            v.tensor_reduce(blk_e[:], blk_ge[:], AX.X, ALU.add).then_inc(v_steps, 1)
            v.wait_ge(v_steps, steps.up(1))
            tt(blk_ge[:], blk_ge[:], by_block(nblk[:]), ALU.mult).then_inc(v_steps, 1)
            v.wait_ge(v_steps, steps.up(1))
            v.tensor_reduce(blk_s[:], blk_ge[:], AX.X, ALU.add).then_inc(v_steps, 1)
            v.wait_ge(v_steps, steps.up(1))
            tt(blk_s[:], blk, blk_s[:], ALU.subtract).then_inc(v_steps, 1)
            v.wait_ge(v_steps, steps.up(1))
            v.tensor_scalar(blk_s[:], blk_s[:], float(P), None, ALU.mult).then_inc(v_steps, 1)
            v.wait_ge(v_steps, steps.up(1))
            v.scalar_tensor_tensor(out=blk_s[:], in0=blk_e[:], scalar=float(REGION), in1=blk_s[:],
                                                   op0=ALU.mult, op1=ALU.add).then_inc(v_steps, 1)
            v.wait_ge(v_steps, steps.up(1))
            v.tensor_scalar(row_tab[:], blk_s[:], float(PAD_ROW), None, ALU.min).then_inc(v_steps, 1)
            steps.up(1)
            v.tensor_scalar(exp_tab[:], blk_e[:], float(NE - 1), float(2 * FF), ALU.min, ALU.mult
            ).then_inc(tables_ready, 1)
            tt(blk_oh[:], by_expert(blk_e[:]), by_block(iota_e), ALU.is_equal).then_inc(v_steps, 1)
            v.wait_ge(v_steps, steps.up(1))

            def ffn(n_x, n_g, n_d):
                if n_x.there:
                    v.wait_ge(f_tx.sem, f_tx.of(n_x))
                    if n_x.has(2):
                        v.wait_ge(f_u.sem, f_u.of(n_x.back(2)))
                    high, low = (xb_T[:, n_x.par % 2, part].rearrange("p c t -> p (c t)") for part in range(2))
                    v.tensor_copy(high, ps_tx[:, 0:2 * P]).then_inc(f_xh.sem, 1)
                    v.wait_ge(f_xh.sem, f_xh.of(n_x))
                    tt(low, ps_tx[:, 0:2 * P], high.bitcast(F32), ALU.subtract).then_inc(f_xT.sem, 1)
                if n_g.there:
                    v.wait_ge(f_silu.sem, f_silu.of(n_g))
                    v.wait_ge(f_u.sem, f_u.of(n_g))
                    if n_g.has(2):
                        v.wait_ge(f_tg.sem, f_tg.of(n_g.back(2)))
                    tt(gu[:, n_g.par % 2], silu[:, n_g.par % 2], ps_u[n_g.par % 2], ALU.mult).then_inc(f_gu.sem, 1)
                if n_d.there:
                    v.wait_ge(xb_in.sems[n_d.par], xb_in.of(n_d))
                    if n_d.has(1):
                        v.wait_ge(f_out.sem, f_out.of(n_d.back(1)))
                    tt(wsel[:], xb[:, n_d.par, ROW_W:ROW_W + NE],
                       blk_oh[:, bass.ds(n_d.index, 1), :].rearrange("p o e -> p (o e)"), ALU.mult).then_inc(f_w, 1)
                    v.wait_ge(f_w, n_d.index * 2 + 1)
                    v.tensor_reduce(wrow[:, 0:1], wsel[:], AX.X, ALU.add).then_inc(f_w, 1)
                    v.wait_ge(f_w, n_d.index * 2 + 2)
                    v.wait_ge(f_y.sem, f_y.of(n_d))
                    if n_d.has(2):
                        v.wait_ge(added.sems[n_d.back(2).par], added.of(n_d.back(2)))
                    v.tensor_scalar(ysb[:, n_d.par % 2], ps_y[n_d.par % 2][:, 0:D], wrow[:, 0:1],
                                                 None, ALU.mult).then_inc(f_out.sem, 1)

            for n in range(PARTS - 1):
                v.wait_ge(low_begun, PARTS + n + 1)
                tt(part_of(wu_low, n), part_of(stage_mem, n), part_of(wu_low, n).bitcast(F32),
                   ALU.subtract).then_inc(low_by_vector, 1)

            v.wait_ge(tables_ready, 1)
            ffn_steps(v, ffn, 0, 1, 2)

        @block.tensor
        def _(pe_):
            pe_.wait_ge(gate_in, GATE_CONSTS)
            for stage, (w, x) in enumerate(((w1_sb, cond_sb), (w2_sb, gh))):
                if stage:
                    pe_.wait_ge(gate_v, 7)
                for c in range(2):
                    for k in range(2):
                        last = pe_.matmul(ps_job[stage][:, c * NB:c * NB + NB], w[:, k, c * P:c * P + P], x[:, k],
                                          start=(k == 0), stop=(k == 1))
                last.then_inc(gate_pe, 1)
            pe_.wait_ge(consts_in, CONSTS)
            pe_.wait_ge(setup_done, SETUP_DONE)
            pe_.wait_ge(gate_v, 7)

            def project(s, name, stage, w, x):
                b = s.batch(stage)
                if b.there:
                    for free, value in bank_free(s, name):
                        pe_.wait_ge(free, value)
                    for c in range(2):
                        for k in range(2):
                            last = pe_.matmul(bank[name][:, c * NT:c * NT + NT], w[:, k, c * P:c * P + P], x(b)[:, k],
                                              start=(k == 0), stop=(k == 1))
                    last.then_inc(pe[name].sem, 1)

            def turn(s, name, stage, x):
                b = s.batch(stage)
                if b.there:
                    for free, value in bank_free(s, name):
                        pe_.wait_ge(free, value)
                    for i in range(2):
                        for j in range(2):
                            last = pe_.transpose(bank[name][:, i * 256 + j * P:i * 256 + j * P + P],
                                                 x(b)[:, j, i * P:i * P + P], ident)
                    last.then_inc(pe[name].sem, 1)

            def outputs(s, g, stage):
                b = s.batch(stage)
                if b.there:
                    pe_.wait_ge(a_exp.sem, a_exp.of(b, 2 * g + 2))
                    if g == 0:
                        pe_.wait_ge(g_v.sem, g_v.of(b))
                    for free, value in bank_free(s, f"pv{g}"):
                        pe_.wait_ge(free, value)
                    for k in range(2):
                        for j in range(4):
                            h = 4 * g + j
                            last = pe_.matmul(bank[f"pv{g}"][32 * j:32 * j + 32, 0:NT], v_aug[:, b.par, NH * k + h],
                                              probs[:, h % 8, k], start=(k == 0), stop=(k == 1))
                    last.then_inc(pe_pv.sem, 1)

            def scores(s, u):
                b = s.batch("att")
                if b.there:
                    if u == 0:
                        pe_.wait_ge(max_loaded.sems[b.par], max_loaded.of(b))
                    if u >= 2:
                        pe_.wait_ge(a_exp.sem, a_exp.of(b, u - 1))
                    else:
                        if b.has(1):
                            pe_.wait_ge(a_exp.sem, a_exp.of(b.back(1), 7 + u))
                    for n in range(2):
                        h = 2 * u + n
                        for k in range(2):
                            last = pe_.matmul(ps_st[u % 2][:, n, k], k_rows[0:SCORE_ROWS, b.par, h, k * P:k * P + P],
                                              q_rows[0:SCORE_ROWS, b.par, h], start=True, stop=True)
                    last.then_inc(pe_st.sem, 1)

            def max_scores(s, h):
                b = s.batch("max")
                if b.there:
                    if h == 0:
                        pe_.wait_ge(rows_loaded.sems[b.par], rows_loaded.of(b))
                    if h >= 2:
                        pe_.wait_ge(v_max.sem, v_max.of(b, h - 1))
                    else:
                        if b.has(1):
                            pe_.wait_ge(v_max.sem, v_max.of(b.back(1), NH - 1 + h))
                    for c in range(2):
                        last = pe_.matmul(ps_sm[h % 2][:, c], q_rows[0:SPLIT_ROWS, b.par, h, c * P:c * P + P],
                                          k_rows[0:SPLIT_ROWS, b.par, h], start=True, stop=True)
                    last.then_inc(pe_sm.sem, 1)

            def turn_outputs(s):
                c = s.batch("out")
                if c.there:
                    pe_.wait_ge(a_ov.sem, a_ov.of(c))
                    for n in range(2):
                        for free, value in bank_free(s, f"tr{n}"):
                            pe_.wait_ge(free, value)
                        for g in range(4):
                            last = pe_.transpose(bank[f"tr{n}"][:, g * P:g * P + P], o_raw[:, g, n * P:n * P + P], ident)
                        last.then_inc(pe_tr.sem, 1)

            def values(s):
                m = s.batch("max")
                if m.there:
                    pe_.wait_ge(v_y.sem, v_y.of(m))
                    for free, value in bank_free(s, "v"):
                        pe_.wait_ge(free, value)
                    for c in range(2):
                        for k in range(2):
                            last = pe_.matmul(bank["v"][:, c * D:c * D + D], y[:, m.par, k, c * P:c * P + P], wv[:, k],
                                              start=(k == 0), stop=(k == 1))
                    last.then_inc(pe["v"].sem, 1)

            def ranks(s):
                e = s.batch("route")
                if e.there:
                    pe_.wait_ge(v_oh.sem, v_oh.of(e))
                    for free, value in bank_free(s, "rank"):
                        pe_.wait_ge(free, value)
                    rank, before, every = bank["rank"], counters[:, 0:P], counters[:, P:2 * P]
                    pe_.matmul(rank[:, 0:2 * NE], before, oh_b[:].rearrange("p c e -> p (c e)"), start=True, stop=False)
                    pe_.matmul(rank[:, NE:2 * NE], every, oh_b[:, 0], start=False, stop=True)
                    pe_.matmul(rank[:, 2 * NE:3 * NE], every, oh_b[:, 0], start=True, stop=False)
                    pe_.matmul(rank[:, 2 * NE:3 * NE], every, oh_b[:, 1], start=False, stop=True
                    ).then_inc(pe["rank"].sem, 1)

            def turn_maxima(s):
                m = s.batch("max")
                if m.there:
                    pe_.wait_ge(v_mx.sem, v_mx.of(m))
                    for free, value in bank_free(s, "mt"):
                        pe_.wait_ge(free, value)
                    for c in range(2):
                        last = pe_.transpose(bank["mt"][0:2 * NH, c * P // 2:c * P // 2 + P // 2].bitcast(BF16),
                                             mx_split[:, c].rearrange("p a h -> p (a h)"), ident_b[:])
                    last.then_inc(pe["mt"].sem, 1)

            def logits(s):
                d = s.batch("rec")
                if d.there:
                    for free, value in bank_free(s, "lg"):
                        pe_.wait_ge(free, value)
                    for c in range(2):
                        for k in range(2):
                            last = pe_.matmul(bank["lg"][:, c * NE:c * NE + NE], hid[:, k, c * P:c * P + P], gw[:, k],
                                              start=(k == 0), stop=(k == 1))
                    last.then_inc(pe["lg"].sem, 1)

            def step(s):
                b, c, d = (s.batch(n) for n in ("qk", "out", "rec"))
                x1_of, y_of = (lambda z: x1[:, z.par]), (lambda z: y[:, z.par])
                if d.there:
                    pe_.wait_ge(v_x1.sem, v_x1.of(d))
                project(s, "f", "rec", wf, x1_of)
                max_scores(s, 0)
                project(s, "i", "rec", wi, x1_of)
                max_scores(s, 1)
                if b.there:
                    pe_.wait_ge(v_y.sem, v_y.of(b))
                project(s, "q", "qk", wq, y_of)
                scores(s, 0)
                max_scores(s, 2)
                max_scores(s, 3)
                outputs(s, 3, "out")
                scores(s, 1)
                turn_outputs(s)
                scores(s, 2)
                max_scores(s, 4)
                max_scores(s, 5)
                project(s, "k", "qk", wk, y_of)
                scores(s, 3)
                outputs(s, 0, "att")
                max_scores(s, 6)
                project(s, "h", "rec", wh, x1_of)
                scores(s, 4)
                max_scores(s, 7)
                values(s)
                max_scores(s, 8)
                max_scores(s, 9)
                scores(s, 5)
                if c.there:
                    pe_.wait_ge(g_o.sem, g_o.of(c))
                turn(s, "aro", "out", lambda z: o_rope)
                scores(s, 6)
                max_scores(s, 10)
                outputs(s, 1, "att")
                scores(s, 7)
                outputs(s, 2, "att")
                max_scores(s, 11)
                ranks(s)
                max_scores(s, 12)
                if c.there:
                    pe_.wait_ge(a_at.sem, a_at.of(c))
                project(s, "wo", "out", wo, lambda z: o_T)
                max_scores(s, 13)
                turn(s, "x1", "rec", x1_of)
                max_scores(s, 14)
                if d.there:
                    pe_.wait_ge(v_hid.sem, v_hid.of(d))
                turn(s, "hid", "rec", lambda z: hid)
                max_scores(s, 15)
                logits(s)
                turn_maxima(s)

            all_steps(pe_, step)

            pe_.wait_ge(tables_ready, 1)

            def ffn(n_x, n_g, n_d):
                if n_g.there:
                    if n_g.i is None and n_g.offset == 0:
                        pe_.wait_ge(down_w_in, 16 * PARTS)
                        pe_.wait_ge(high_made, 2 * PARTS)
                    at = pe_.value_load(exp_tab[0:1, bass.ds(n_g.index, 1)], min_val=0, max_val=(NE - 1) * 2 * FF)
                    pe_.wait_ge(f_xT.sem, f_xT.of(n_g))
                    if n_g.has(2):
                        pe_.wait_ge(f_silu.sem, f_silu.of(n_g.back(2)))
                    if n_g.has(2):
                        pe_.wait_ge(f_gu.sem, f_gu.of(n_g.back(2)))
                    for k in range(2):
                        for n, (part, w) in enumerate(((0, wg_high), (0, wg_low), (1, wg_high))):
                            last = pe_.matmul(ps_g[n_g.par % 2], xb_T[:, n_g.par % 2, part, k],
                                              w[:, bass.ds(at + k * FF, FF)],
                                              start=(k == 0 and n == 0), stop=(k == 1 and n == 2))
                    last.then_inc(f_g.sem, 1)
                if n_d.there:
                    pe_.wait_ge(f_gu.sem, f_gu.of(n_d))
                    if n_d.has(1):
                        pe_.wait_ge(f_guT.sem, f_guT.of(n_d.back(1)))
                    for k in range(4):
                        last = pe_.transpose(ps_tg[:, k * P:k * P + P], gu[:, n_d.par % 2, k * P:k * P + P], ident)
                    last.then_inc(f_tg.sem, 1)
                if n_g.there:
                    for k in range(2):
                        for n, (part, w) in enumerate(((0, wu_high), (0, wu_low), (1, wu_high))):
                            last = pe_.matmul(ps_u[n_g.par % 2], xb_T[:, n_g.par % 2, part, k],
                                              w[:, bass.ds(at + k * FF, FF)],
                                              start=(k == 0 and n == 0), stop=(k == 1 and n == 2))
                    last.then_inc(f_u.sem, 1)
                if n_x.there:
                    pe_.wait_ge(xb_in.sems[n_x.par], xb_in.of(n_x))
                    if n_x.has(1):
                        pe_.wait_ge(f_xT.sem, f_xT.of(n_x.back(1)))
                    for k in range(2):
                        last = pe_.transpose(ps_tx[:, k * P:k * P + P], xb[:, n_x.par, k * P:k * P + P], ident)
                    last.then_inc(f_tx.sem, 1)
                if n_d.there:
                    at = pe_.value_load(exp_tab[0:1, bass.ds(n_d.index, 1)], min_val=0, max_val=(NE - 1) * 2 * FF)
                    pe_.wait_ge(f_guT.sem, f_guT.of(n_d))
                    if n_d.has(2):
                        pe_.wait_ge(f_out.sem, f_out.of(n_d.back(2)))
                    for k in range(4):
                        last = pe_.matmul(ps_y[n_d.par % 2][:, 0:D], gu_T[:, k], wd_all[:, bass.ds(at + k * D, D)],
                                          start=(k == 0), stop=(k == 3))
                    last.then_inc(f_y.sem, 1)

            ffn_steps(pe_, ffn, 0, 1, 2)


def by_partition(a):
    return np.ascontiguousarray(a.reshape(-1, P, a.shape[-1]).transpose(1, 0, 2))


def kernel(**inputs):
    import concourse.bacc as bacc
    from concourse.bass_utils import run_bass_kernel_spmd

    a = {n: np.asarray(v) for n, v in inputs.items()}
    def qk_order(w):
        return w.reshape(NH, HALF, 2, -1).transpose(2, 1, 0, 3).reshape(D, -1)

    def v_order(w):
        return w.reshape(NH, HALF, 2, -1).transpose(2, 0, 1, 3).reshape(D, -1)

    def weight(w):
        return by_partition(w.T)

    def column(b):
        return np.ascontiguousarray(b.reshape(2, P).T)

    cos, sin = rope_tables()
    cs = np.stack([cos, sin])
    by_pair = np.repeat(cs.transpose(0, 2, 1), NH, axis=1)
    rope_qk = np.stack([by_pair, by_pair[::-1]]).transpose(2, 0, 1, 3).reshape(P, -1)
    v_tab = np.tile(cs.transpose(1, 0, 2).reshape(2, P, 2, 1, HALF), (1, 1, 1, NH, 1))
    rope_v = np.stack([v_tab, v_tab[:, :, ::-1]]).transpose(2, 0, 1, 3, 4, 5).reshape(P, -1)
    o_tab = np.stack([np.stack([-cos, sin], -1), np.stack([-sin, -cos], -1)])
    o_tab = np.tile(o_tab.reshape(2, 2, P, 1, HD), (1, 1, 1, NH, 1))
    rope_out = o_tab.transpose(2, 0, 1, 3, 4).reshape(P, -1)
    small = {
        "bias": np.stack([column(b) for b in (qk_order(a["L0_attn_bq"]), qk_order(a["L0_attn_bk"]), a["L0_attn_bo"],
                                              a["L0_cond2_b_f"], a["L0_cond2_b_i"], a["L0_cond2_b_h"],
                                              a["L0_cond_b1"], a["L0_cond_b2"])], 1),
        "gate_w": by_partition(a["L0_ffn_gate_w"]),
        "cond": by_partition(a["cond_1024"].T),
        "bv": np.broadcast_to(v_order(a["L0_attn_bv"]).reshape(1, D), (P, D)),
        "blocks": np.broadcast_to(np.arange(NBLK, dtype=np.float32), (P, NBLK)),
        "ident": np.eye(P, dtype=np.float32),
        "upper": np.triu(np.ones((P, P), np.float32), 1),
        "ones": np.ones((P, P), np.float32),
        "iota_e": np.broadcast_to(np.arange(NE, dtype=np.float32), (P, NE)),
        "region_e": np.broadcast_to(np.arange(NE, dtype=np.float32) * REGION, (P, NE)),
        "token_p": (np.arange(P)[:, None] + np.array([0, P])[None, :]).astype(np.float32),
    }

    def together(*parts):
        return np.concatenate([p.reshape(P, -1) for p in parts], 1)

    arrays = {
        "xT": a["x"].transpose(2, 0, 1),
        "gate_weights": together(weight(a["L0_cond_W1"]), weight(a["L0_cond_W2"])),
        "small": together(*(small[name] for name in SMALL_SIZES)),
        "early_weights": together(weight(qk_order(a["L0_attn_Wq"])), weight(qk_order(a["L0_attn_Wk"])),
                                  weight(v_order(a["L0_attn_Wv"])), rope_qk),
        "late_weights": together(*(weight(a[n]) for n in ("L0_attn_Wo", "L0_cond2_W_f", "L0_cond2_W_i",
                                                          "L0_cond2_W_h"))),
        "rope_tokens": together(rope_v, rope_out),
        "w_gate": a["L0_ffn_gate_proj_w"].reshape(NE, 2, P, FF).transpose(2, 0, 1, 3).reshape(P, -1),
        "w_up": a["L0_ffn_up_proj_w"].reshape(NE, 2, P, FF).transpose(2, 0, 1, 3).reshape(P, -1),
        "w_down": a["L0_ffn_down_proj_w"].reshape(NE, 4, P, D).transpose(2, 0, 1, 3).reshape(P, -1),
    }
    arrays = {f"in_{n}": np.ascontiguousarray(v) for n, v in arrays.items()}
    nc = bacc.Bacc("TRN2", target_bir_lowering=False, num_devices=1)
    args = {n[3:]: nc.dram_tensor(n, v.shape, mybir.dt.from_np(v.dtype), kind="ExternalInput").ap()
            for n, v in arrays.items()}
    out = nc.dram_tensor("out_rows", (TOKENS + P, D), F32, kind="ExternalOutput").ap()
    build(nc, out=out, **args)
    result = run_bass_kernel_spmd(nc, [arrays], core_ids=[0]).results[0]["out_rows"]
    return result[:TOKENS].reshape(NB, NT, D)
```
